# Optimizing a Trainium2 kernel written in Bass

```python
import numpy as np
import jax
import jax.numpy as jnp

def _softmax(x, axis=-1):
    return jax.nn.softmax(x, axis=axis)

def _gelu(x):
    return jax.nn.gelu(x, approximate=True)

def _silu(x):
    return jax.nn.silu(x)

def _sigmoid(x):
    return jax.nn.sigmoid(x)

def _layernorm(x, axis=-1, eps=1e-05):
    m = jnp.mean(x, axis=axis, keepdims=True)
    v = jnp.var(x, axis=axis, keepdims=True)
    return (x - m) / jnp.sqrt(v + eps)

def _scatter_add(tgt, idx, src, axis=0):
    return tgt.at[idx].add(src)

def _segment_sum(src, seg, n):
    return jax.ops.segment_sum(src, seg, n)
kernel_name = 'mk_gnn_preln_d4_gnn_r16_56ef97'

def setup_inputs(seed: int=0):
    np.random.seed(seed)
    _w = jnp.asarray

    def _rec_inputs():
        import jax
        import jax.numpy as jnp
        _gk = jax.random.key(seed)
        x = -0.000202 + 1 * jax.random.normal(jax.random.fold_in(_gk, 1), (3125, 128), jnp.float32)
        src = jax.random.randint(jax.random.fold_in(_gk, 2), (100000,), 0, 3125, jnp.int32)
        dst = jax.random.randint(jax.random.fold_in(_gk, 3), (100000,), 0, 3125, jnp.int32)
        _o = jnp.argsort(dst, stable=True)
        src = src[_o]
        dst = dst[_o]
        edge_weight = jax.random.uniform(jax.random.fold_in(_gk, 14), (100000,), jnp.float32, 0.0, 0.999998)
        return (x, src, dst, edge_weight)
    x, src, dst, edge_weight = _rec_inputs()

    def _L0_gnn_setup():
        import jax, jax.numpy as jnp
        import numpy as np
        N_NODES = 3125
        N_EDGES = 50000
        H = 128
        T = 2
        key = jax.random.key(seed)
        ks = jax.random.split(key, 8)
        s = 0.05
        return {'h': jax.random.normal(ks[0], (N_NODES, H), jnp.float32), 'edges': jax.random.randint(ks[1], (N_EDGES, 2), 0, N_NODES, jnp.int64), 'W_msg': jax.random.normal(ks[2], (T, 2 * H, 2 * H), jnp.float32) * s, 'b_msg': jax.random.normal(ks[3], (T, 2 * H), jnp.float32) * s, 'W_ih': jax.random.normal(ks[4], (T, 3 * H, 2 * H), jnp.float32) * s, 'W_hh': jax.random.normal(ks[5], (T, 3 * H, H), jnp.float32) * s, 'b_ih': jax.random.normal(ks[6], (T, 3 * H), jnp.float32) * s, 'b_hh': jax.random.normal(ks[7], (T, 3 * H), jnp.float32) * s}
    _L0_gnn_all = _L0_gnn_setup()
    _L0_gnn_in = {k: v for k, v in _L0_gnn_all.items() if k in ('W_msg', 'b_msg', 'W_ih', 'W_hh', 'b_ih', 'b_hh')}
    del _L0_gnn_all

    def _L1_gnn_setup():
        import jax, jax.numpy as jnp
        import numpy as np
        N_NODES = 6250
        N_EDGES = 37500
        D_IN = 128
        D_OUT = 128
        key = jax.random.key(seed)
        k1, k2, k3, k4 = jax.random.split(key, 4)
        x = jax.random.normal(k1, (N_NODES, D_IN), dtype=jnp.float32)
        edge_index = jax.random.randint(k2, (2, N_EDGES), 0, N_NODES, dtype=jnp.int64)
        edge_weight = jax.random.uniform(k3, (N_EDGES,), dtype=jnp.float32)
        W = jax.random.normal(k4, (D_IN, D_OUT), dtype=jnp.float32) * (1.0 / np.sqrt(D_IN))
        b = jnp.zeros((D_OUT,), dtype=jnp.float32)
        return {'x': x, 'edge_index': edge_index, 'edge_weight': edge_weight, 'W': W, 'b': b}
    _L1_gnn_all = _L1_gnn_setup()
    _L1_gnn_in = {k: v for k, v in _L1_gnn_all.items() if k in ('W', 'b')}
    del _L1_gnn_all

    def _L2_gnn_setup():
        import jax, jax.numpy as jnp
        import numpy as np
        N_NODES = 3125
        N_EDGES = 50000
        IN_FEATS = 128
        HEADS = 4
        OUT_FEATS = 32
        NEG_SLOPE = 0.2

        def _edge_softmax(e, dst, n_nodes):
            seg_max = jax.ops.segment_max(e, dst, num_segments=n_nodes)
            ex = jnp.exp(e - seg_max[dst])
            seg_sum = jax.ops.segment_sum(ex, dst, num_segments=n_nodes)
            return ex / seg_sum[dst]
        key = jax.random.key(seed)
        ks = jax.random.split(key, 9)
        HD = HEADS * OUT_FEATS
        return {'feat': jax.random.normal(ks[0], (N_NODES, IN_FEATS), dtype=jnp.float32), 'W_src': jax.random.normal(ks[1], (HD, IN_FEATS), dtype=jnp.float32) * (1.0 / np.sqrt(IN_FEATS)), 'b_src': jax.random.normal(ks[2], (HD,), dtype=jnp.float32) * 0.02, 'W_dst': jax.random.normal(ks[3], (HD, IN_FEATS), dtype=jnp.float32) * (1.0 / np.sqrt(IN_FEATS)), 'b_dst': jax.random.normal(ks[4], (HD,), dtype=jnp.float32) * 0.02, 'W_v': jax.random.normal(ks[5], (HD, IN_FEATS), dtype=jnp.float32) * (1.0 / np.sqrt(IN_FEATS)), 'b_v': jax.random.normal(ks[6], (HD,), dtype=jnp.float32) * 0.02, 'src': jax.random.randint(ks[7], (N_EDGES,), 0, N_NODES, dtype=jnp.int32), 'dst': jax.random.randint(ks[8], (N_EDGES,), 0, N_NODES, dtype=jnp.int32)}
    _L2_gnn_all = _L2_gnn_setup()
    _L2_gnn_in = {k: v for k, v in _L2_gnn_all.items() if k in ('W_src', 'b_src', 'W_dst', 'b_dst', 'W_v', 'b_v')}
    del _L2_gnn_all

    def _L3_gnn_setup():
        import jax, jax.numpy as jnp
        import numpy as np
        N_NODES = 6250
        N_EDGES = 100000
        D_IN = 128
        D_HID = 128
        D_OUT = 128
        key = jax.random.key(seed)
        ks = jax.random.split(key, 8)
        s = lambda d: 1.0 / np.sqrt(d)
        return {'x': jax.random.normal(ks[0], (N_NODES, D_IN), dtype=jnp.float32), 'edge_src': jax.random.randint(ks[1], (N_EDGES,), 0, N_NODES, dtype=jnp.int64), 'edge_dst': jax.random.randint(ks[2], (N_EDGES,), 0, N_NODES, dtype=jnp.int64), 'W1': jax.random.normal(ks[3], (D_IN, D_HID), dtype=jnp.float32) * s(D_IN), 'b1': jnp.zeros((D_HID,), dtype=jnp.float32), 'W_self': jax.random.normal(ks[4], (D_HID, D_HID), dtype=jnp.float32) * s(D_HID), 'W_neigh': jax.random.normal(ks[5], (D_HID, D_HID), dtype=jnp.float32) * s(D_HID), 'b_sage': jnp.zeros((D_HID,), dtype=jnp.float32), 'W2': jax.random.normal(ks[6], (D_HID, D_OUT), dtype=jnp.float32) * s(D_HID), 'b2': jnp.zeros((D_OUT,), dtype=jnp.float32)}
    _L3_gnn_all = _L3_gnn_setup()
    _L3_gnn_in = {k: v for k, v in _L3_gnn_all.items() if k in ('W1', 'b1', 'W_self', 'W_neigh', 'b_sage', 'W2', 'b2')}
    del _L3_gnn_all
    return {'x': x, 'src': src, 'dst': dst, 'edge_weight': edge_weight, 'L0_gnn_W_msg': _L0_gnn_in['W_msg'], 'L0_gnn_b_msg': _L0_gnn_in['b_msg'], 'L0_gnn_W_ih': _L0_gnn_in['W_ih'], 'L0_gnn_W_hh': _L0_gnn_in['W_hh'], 'L0_gnn_b_ih': _L0_gnn_in['b_ih'], 'L0_gnn_b_hh': _L0_gnn_in['b_hh'], 'L1_gnn_W': _L1_gnn_in['W'], 'L1_gnn_b': _L1_gnn_in['b'], 'L2_gnn_W_src': _L2_gnn_in['W_src'], 'L2_gnn_b_src': _L2_gnn_in['b_src'], 'L2_gnn_W_dst': _L2_gnn_in['W_dst'], 'L2_gnn_b_dst': _L2_gnn_in['b_dst'], 'L2_gnn_W_v': _L2_gnn_in['W_v'], 'L2_gnn_b_v': _L2_gnn_in['b_v'], 'L3_gnn_W1': _L3_gnn_in['W1'], 'L3_gnn_b1': _L3_gnn_in['b1'], 'L3_gnn_W_self': _L3_gnn_in['W_self'], 'L3_gnn_W_neigh': _L3_gnn_in['W_neigh'], 'L3_gnn_b_sage': _L3_gnn_in['b_sage'], 'L3_gnn_W2': _L3_gnn_in['W2'], 'L3_gnn_b2': _L3_gnn_in['b2']}

def reference(x, src, dst, edge_weight, L0_gnn_W_msg, L0_gnn_b_msg, L0_gnn_W_ih, L0_gnn_W_hh, L0_gnn_b_ih, L0_gnn_b_hh, L1_gnn_W, L1_gnn_b, L2_gnn_W_src, L2_gnn_b_src, L2_gnn_W_dst, L2_gnn_b_dst, L2_gnn_W_v, L2_gnn_b_v, L3_gnn_W1, L3_gnn_b1, L3_gnn_W_self, L3_gnn_W_neigh, L3_gnn_b_sage, L3_gnn_W2, L3_gnn_b2):
    import jax
    import jax.numpy as jnp

    def _L0_gnn_ref(h, edges, W_msg, b_msg, W_ih, W_hh, b_ih, b_hh):
        import jax, jax.numpy as jnp
        import numpy as np
        N_NODES = 3125
        N_EDGES = 50000
        H = 128
        T = 2
        n_nodes, hd = h.shape
        src, dst = (edges[:, 0], edges[:, 1])
        deg = jax.ops.segment_sum(jnp.ones(edges.shape[0], h.dtype), dst, num_segments=n_nodes)
        has_msg = (deg > 0)[:, None]
        for t in range(W_msg.shape[0]):
            m_in = jnp.concatenate([h[src], h[dst]], axis=-1)
            m = m_in @ W_msg[t].T + b_msg[t]
            agg = jax.ops.segment_sum(m, dst, num_segments=n_nodes)
            gi = agg @ W_ih[t].T + b_ih[t]
            gh = h @ W_hh[t].T + b_hh[t]
            ir, iz, inn = (gi[:, :hd], gi[:, hd:2 * hd], gi[:, 2 * hd:])
            hr, hz, hn = (gh[:, :hd], gh[:, hd:2 * hd], gh[:, 2 * hd:])
            r = jax.nn.sigmoid(ir + hr)
            z = jax.nn.sigmoid(iz + hz)
            n = jnp.tanh(inn + r * hn)
            h_new = (1.0 - z) * n + z * h
            h = jnp.where(has_msg, h_new, h)
        return h

    def _L1_gnn_ref(x, edge_index, edge_weight, W, b):
        import jax, jax.numpy as jnp
        import numpy as np
        N_NODES = 6250
        N_EDGES = 37500
        D_IN = 128
        D_OUT = 128
        N = x.shape[0]
        x = x.astype(jnp.float32)
        loop = jnp.arange(N, dtype=edge_index.dtype)
        row = jnp.concatenate([edge_index[0], loop])
        col = jnp.concatenate([edge_index[1], loop])
        w = jnp.concatenate([edge_weight, jnp.ones((N,), dtype=x.dtype)])
        deg = jax.ops.segment_sum(w, col, num_segments=N)
        deg_inv_sqrt = jnp.where(deg > 0, jax.lax.rsqrt(deg), 0.0)
        norm = deg_inv_sqrt[row] * w * deg_inv_sqrt[col]
        xw = x @ W
        msgs = norm[:, None] * xw[row]
        out = jax.ops.segment_sum(msgs, col, num_segments=N) + b
        return out

    def _L2_gnn_ref(feat, W_src, b_src, W_dst, b_dst, W_v, b_v, src, dst):
        import jax, jax.numpy as jnp
        import numpy as np
        N_NODES = 3125
        N_EDGES = 50000
        IN_FEATS = 128
        HEADS = 4
        OUT_FEATS = 32
        NEG_SLOPE = 0.2

        def _edge_softmax(e, dst, n_nodes):
            seg_max = jax.ops.segment_max(e, dst, num_segments=n_nodes)
            ex = jnp.exp(e - seg_max[dst])
            seg_sum = jax.ops.segment_sum(ex, dst, num_segments=n_nodes)
            return ex / seg_sum[dst]
        n = feat.shape[0]
        f_src = (feat @ W_src.T + b_src).reshape(n, HEADS, OUT_FEATS)
        f_dst = (feat @ W_dst.T + b_dst).reshape(n, HEADS, OUT_FEATS)
        f_v = (feat @ W_v.T + b_v).reshape(n, HEADS, OUT_FEATS)
        a = f_src[src] + f_dst[dst]
        e = jnp.where(a >= 0, a, NEG_SLOPE * a)
        sa = _edge_softmax(e, dst, n)
        m = f_v[src] * sa
        rst = jax.ops.segment_sum(m, dst, num_segments=n)
        return rst.reshape(n, HEADS * OUT_FEATS)

    def _L3_gnn_ref(x, edge_src, edge_dst, W1, b1, W_self, W_neigh, b_sage, W2, b2):
        import jax, jax.numpy as jnp
        import numpy as np
        N_NODES = 6250
        N_EDGES = 100000
        D_IN = 128
        D_HID = 128
        D_OUT = 128
        n_dst = x.shape[0]
        h = jax.nn.relu(x @ W1 + b1)
        msg = h[edge_src]
        neigh_sum = jax.ops.segment_sum(msg, edge_dst, num_segments=n_dst)
        deg = jax.ops.segment_sum(jnp.ones((edge_dst.shape[0],), h.dtype), edge_dst, num_segments=n_dst)
        h_neigh = neigh_sum / jnp.maximum(deg, 1.0)[:, None]
        h2 = jax.nn.relu(h @ W_self + h_neigh @ W_neigh + b_sage)
        return jax.nn.relu(h2 @ W2 + b2)
    edge_index = jnp.stack([src, dst])
    edge_index_t = jnp.stack([src, dst], axis=1)
    h = jnp.maximum(_layernorm(x, axis=-1), 0.0)
    x = x + _L0_gnn_ref(h, edge_index_t, L0_gnn_W_msg, L0_gnn_b_msg, L0_gnn_W_ih, L0_gnn_W_hh, L0_gnn_b_ih, L0_gnn_b_hh)
    h = jnp.maximum(_layernorm(x, axis=-1), 0.0)
    x = x + _L1_gnn_ref(h, edge_index, edge_weight, L1_gnn_W, L1_gnn_b)
    h = jnp.maximum(_layernorm(x, axis=-1), 0.0)
    x = x + _L2_gnn_ref(h, L2_gnn_W_src, L2_gnn_b_src, L2_gnn_W_dst, L2_gnn_b_dst, L2_gnn_W_v, L2_gnn_b_v, src, dst)
    h = jnp.maximum(_layernorm(x, axis=-1), 0.0)
    x = x + _L3_gnn_ref(h, src, dst, L3_gnn_W1, L3_gnn_b1, L3_gnn_W_self, L3_gnn_W_neigh, L3_gnn_b_sage, L3_gnn_W2, L3_gnn_b2)
    return x

_drawn_inputs = setup_inputs


def setup_inputs(seed=0):
    import zlib

    import numpy as np

    out = dict(_drawn_inputs(seed))
    spreads = {'L1_gnn_b': (0.0, 0.1),
     'L3_gnn_b1': (0.0, 0.287),
     'L3_gnn_b_sage': (0.0, 0.291),
     'L3_gnn_b2': (0.0, 0.1)}
    factors = {'L0_gnn_b_ih': 3.135,
     'L0_gnn_b_hh': 4.685,
     'L2_gnn_b_src': 8.0,
     'L2_gnn_W_dst': 4.736,
     'L2_gnn_b_dst': 8.0,
     'L2_gnn_b_v': 4.036}
    for name, (base, spread) in spreads.items():
        noise = np.random.default_rng([zlib.crc32(name.encode()), seed]).standard_normal(out[name].shape)
        drawn = base * np.exp(spread * noise) if base else spread * noise
        out[name] = jnp.asarray(drawn.astype(out[name].dtype))
    for name, factor in factors.items():
        out[name] = (out[name] * factor).astype(out[name].dtype)
    return out
```

```python
import concourse.bass as bass
from concourse import mybir
from contextlib import ExitStack

N = 3125
E = 100000
P = 128
F = 128
NBR = -(-N // P)
NB = 28
NG = NB // 4
TAIL = N - (NBR - 1) * P
TILE = 128
CT = 4
CE = CT * TILE
NC = 196
R = 4
IT = NC // R
EB = 7
TR = EB * P
FULL = E // TILE
REST = E - FULL * TILE
BIG = 1e30
EPS = 1e-5
NONE = 4096


def build(nc, a, out):
    f32, bf16, i32 = mybir.dt.float32, mybir.dt.bfloat16, mybir.dt.int32
    ALU, ACT, AX = mybir.AluOpType, mybir.ActivationFunctionType, mybir.AxisListType
    ctx = ExitStack()
    with ctx:
        def sb(name, shape, dt=f32):
            return ctx.enter_context(nc.sbuf_tensor(name, shape, dt))

        def sem(name):
            return ctx.enter_context(nc.semaphore(name))

        def dram(name, shape, dt=f32):
            return nc.dram_tensor(name, shape, dt).ap()

        dst_rows = dram("dst_rows", (TR + 1, TILE), i32)
        keep_d = dram("keep_d", (TR * TILE,), bf16)
        cut_d = dram("cut_d", (TR * TILE,), bf16)
        wsum_d = dram("wsum_d", (TR * TILE, 1))
        tabs = [dram(f"tab{p}", (NB * P, F)) for p in range(4)]
        tab_sv = dram("tab_sv", (NB * P, 2 * F))
        tab_d = dram("tab_d", (NB * P, F))
        run_d = dram("run_d", (NC * CE, F))

        X = sb("X", [P, NB, F])
        H = sb("H", [P, NB, F])
        A = sb("A", [P, NB, F])
        V = sb("V", [P, NB, F])
        HTx = sb("HTx", [P, NB * P + 1])
        HT = HTx[:, 0:NB * P]
        AT = V[:, :, :].rearrange("p b c -> p (b c)")
        VT = sb("VT", [P, NB * P])
        NWB = 29
        WT = sb("WT", [P, NWB, P])
        WD = sb("WD", [P, 5, P])
        brow = sb("brow", [1, 2 * 1024 + 512])
        bcol = sb("bcol", [P, 2])
        b1bc = sb("b1bc", [P, F])
        ident = sb("ident", [P, P])
        ones = sb("ones", [P, P])
        dst_i, src_i, w_t, dst_f = (VT[:, k * TR:(k + 1) * TR].rearrange("p (b e) -> p b e", e=TILE) for k in range(4))
        dst_i, src_i = dst_i.bitcast(i32), src_i.bitcast(i32)
        src_e = sb("src_e", [P, TR])
        dst_e = sb("dst_e", [P, TR])
        w_e = sb("w_e", [P, TR])
        prev_i = sb("prev_i", [P, EB], i32)
        noprev = sb("noprev", [1, TILE], i32)
        prev_f = sb("prev_f", [P, EB])
        zero = sb("zero", [P, TILE], bf16)
        keep_t = sb("keep_t", [P, EB, TILE], bf16)
        cut_t = sb("cut_t", [P, EB, TILE], bf16)
        nval = sb("nval", [P, NB])
        nval_i = sb("nval_i", [P, NB], i32)
        cnt = sb("cnt", [P, NB])
        cnt2 = sb("cnt2", [P, NB])
        trow = sb("trow", [P, NB])
        trow_i = sb("trow_i", [P, NB], i32)
        cum = sb("cum", [P, NB])
        last_i = sb("last_i", [P, NB], i32)
        deg = sb("deg", [P, NB])
        has = sb("has", [P, NB])
        invdeg = sb("invdeg", [P, NB])
        wlast = sb("wlast", [P, NB])
        dis = sb("dis", [P, NB])
        tmpn = sb("tmpn", [P, NB])
        mean = sb("mean", [P, NB])
        rstd = sb("rstd", [P, NB])
        tails = HTx[0:1, 0:2 * TR].rearrange("p (u t) -> p u t", u=2)
        carry = HTx[0:1, 2 * TR:3 * TR + 1]
        cprev = sb("cprev", [P, EB])
        row = HTx[0:1, :]
        degrow = sb("degrow", [1, NB * P])
        stage = sb("stage", [P, R, 2, CT], i32)
        G = sb("G", [P, R, CT, 3 * F])
        mring = sb("mring", [P, R, CE], bf16)
        ST = sb("ST", [P, 2, CE])
        OS = sb("OS", [P, 2, CE])
        RB = sb("RB", [P, 2, CE + 1])
        D01 = sb("D01", [P, 2, 2 * CE])
        DN = sb("DN", [P, 2, CE])
        NN = sb("NN", [P, 2, CE])
        M2 = sb("M2", [P, 2, 2, 512])
        Ee, NV = M2[:, 0, :, :], M2[:, 1, :, :]
        big = G[:, :, :, :].rearrange("p a b c -> p (a b c)")
        rgate = D01[:, 0, 0:512]
        omz = D01[:, 0, 512:1024]
        cand = D01[:, 1, 0:512]
        tnh = D01[:, 1, 512:1024]
        WN = big[:, 0:NWB * P].rearrange("p (b c) -> p b c", c=P)
        EV = big[:, 0:2 * 4 * 384].rearrange("p (s k c) -> p s k c", s=2, c=384)
        P_t = V[:, 0:EB, :]
        lead = V[:, EB:2 * EB, :]
        fbc = V[:, 2 * EB:3 * EB, :]
        S_t = V[:, 3 * EB:4 * EB, :]
        rows_i = A[:, :, :].bitcast(i32)
        junk = H[:, 0:EB, :].rearrange("p b e -> p (b e)")
        dclip = H[:, EB:2 * EB, :]
        src_f = H[:, 2 * EB:3 * EB, :]

        PS = ctx.enter_context(nc.psum_tensor("PS", [P, 8, 512], f32))

        cleared = sem("cleared")
        ld = sem("ld")
        ldw = sem("ldw")
        dpad = sem("dpad")
        prevld = sem("prevld")
        setup = sem("setup")
        cst = sem("cst")
        pst = sem("pst")
        maskst = sem("maskst")
        rowg = sem("rowg")
        wg = sem("wg")
        sq = sem("sq")
        h_ready = sem("h_ready")
        lnv = sem("lnv")
        lns = sem("lns")
        nstep = sem("nstep")
        tr = sem("tr")
        tre = sem("tre")
        v_ready = sem("v_ready")
        a_ready = sem("a_ready")
        agg = sem("agg")
        tabst = sem("tabst")
        attst = [sem(f"attst{q}") for q in range(2)]
        mm = sem("mm")
        mev = sem("mev")
        gr = sem("gr")
        gact = sem("gact")
        gdve = sem("gdve")
        osem = sem("osem")
        zsem = sem("zsem")
        turn = sem("turn")
        staged = sem("staged")
        gath = [sem(f"gath{h}") for h in range(R)]
        scaled = sem("scaled")
        xt = sem("xt")
        scan = sem("scan")
        back = sem("back")
        ev = sem("ev")
        odma = [sem(f"odma{q}") for q in range(2)]
        mld = [sem(f"mld{h}") for h in range(R)]
        ga = sem("ga")
        ge = sem("ge")
        gx = sem("gx")
        gchain = sem("gchain")
        gstaged = sem("gstaged")
        ggath = [sem(f"ggath{h}") for h in range(R)]
        block = ctx.enter_context(nc.Block())

        SUM = [0, 1, 2, 4]

        def blocks_of(t):
            b = [("L0_gnn_W_msg", t, q, m) for q in range(2) for m in range(2)]
            b += [("L0_gnn_W_ih", t, q, m) for q in range(3) for m in range(2)]
            return b + [("L0_gnn_W_hh", t, q, 0) for q in range(3)]

        def BM(t): return t * 1024
        def BI(t): return t * 1024 + 256
        def BH(t): return t * 1024 + 640
        BQ = 2048
        B2 = 2048 + 384

        def fori(eng, p, body):
            if p == 0:
                body(0, True)
                with eng.Fori(1, IT) as i:
                    body(i, False)
            else:
                with eng.Fori(0, IT) as i:
                    body(i, False)

        @block.sync
        def _(sp):
            for t in range(2):
                o = t * 13
                sp.dma_start(WN[:, o:o + 4, :], a["L0_gnn_W_msg"][t].rearrange("(q p) (m c) -> p q m c", p=P, c=P)).then_inc(ldw, 16)
                sp.dma_start(WN[:, o + 4:o + 10, :], a["L0_gnn_W_ih"][t].rearrange("(q p) (m c) -> p q m c", p=P, c=P)).then_inc(ldw, 16)
                sp.dma_start(WN[:, o + 10:o + 13, :], a["L0_gnn_W_hh"][t].rearrange("(q p) c -> p q c", p=P)).then_inc(ldw, 16)
                sp.dma_start(brow[0:1, BM(t):BM(t) + 256], a["L0_gnn_b_msg"][t:t + 1, :]).then_inc(ldw, 16)
                sp.dma_start(brow[0:1, BI(t):BI(t) + 384], a["L0_gnn_b_ih"][t:t + 1, :]).then_inc(ldw, 16)
                sp.dma_start(brow[0:1, BH(t):BH(t) + 384], a["L0_gnn_b_hh"][t:t + 1, :]).then_inc(ldw, 16)
            for k, s in enumerate(("src", "v", "dst")):
                sp.dma_start(WN[:, 26 + k, :], a[f"L2_gnn_W_{s}"]).then_inc(ldw, 16)
                sp.dma_start(brow[0:1, BQ + k * P:BQ + k * P + P], a[f"L2_gnn_b_{s}"].rearrange("(o f) -> o f", o=1)).then_inc(ldw, 16)
            for k, s in enumerate(("L1_gnn_W", "L3_gnn_W1", "L3_gnn_W_self", "L3_gnn_W_neigh", "L3_gnn_W2")):
                sp.dma_start(WD[:, k, :], a[s]).then_inc(ldw, 16)
            sp.dma_start(brow[0:1, B2:B2 + P], a["L3_gnn_b2"].rearrange("(o f) -> o f", o=1)).then_inc(ldw, 16)
            sp.dma_start(bcol[:, 0:1], a["L3_gnn_b1"].rearrange("(f o) -> f o", o=1)).then_inc(ldw, 16)
            sp.dma_start(bcol[:, 1:2], a["L3_gnn_b_sage"].rearrange("(f o) -> f o", o=1)).then_inc(ldw, 16)
            sp.dma_start(b1bc[:, :], a["L1_gnn_b"].partition_broadcast(P)).then_inc(ldw, 16)
            sp.wait_ge(cleared, 4)
            for tile, name in ((dst_i, "dst"), (src_i, "src"), (w_t, "edge_weight")):
                nfull = FULL // P
                sp.dma_start(tile[:, 0:nfull, :], a[name][0:nfull * P * TILE].rearrange("(b p e) -> p b e", p=P, e=TILE)).then_inc(ld, 16)
                sp.dma_start(tile[0:FULL - nfull * P, nfull, :], a[name][nfull * P * TILE:FULL * TILE].rearrange("(p e) -> p e", e=TILE)).then_inc(ld, 16)
                sp.dma_start(tile[FULL - nfull * P:FULL - nfull * P + 1, nfull, 0:REST], a[name][FULL * TILE:E].rearrange("(o e) -> o e", o=1)).then_inc(ld, 16)
            sp.dma_start(X[:, 0:NBR - 1, :], a["x"][0:(NBR - 1) * P, :].rearrange("(j p) f -> p j f", p=P)).then_inc(ld, 16)
            sp.dma_start(X[0:TAIL, NBR - 1, :], a["x"][(NBR - 1) * P:N, :]).then_inc(ld, 16)
            sp.wait_ge(ld, 16 * 11)
            sp.dma_start(dst_rows[1:TR + 1, :].rearrange("(b p) e -> p b e", p=P), dst_i[:, :, :]).then_inc(dpad, 16)
            sp.dma_start(dst_rows[0:1, :], noprev[:, :]).then_inc(dpad, 16)
            sp.wait_ge(dpad, 32)
            sp.dma_start(prev_i[:, :], dst_rows[0:TR, TILE - 1:TILE].rearrange("(b p) o -> p (b o)", p=P), allow_slow_non_contiguous=True).then_inc(prevld, 16)
            sp.wait_ge(setup, 5)
            sp.dma_start(keep_d.rearrange("(b p e) -> p b e", p=P, e=TILE), keep_t[:, :, :]).then_inc(maskst, 16)
            sp.dma_start(cut_d.rearrange("(b p e) -> p b e", p=P, e=TILE), cut_t[:, :, :]).then_inc(maskst, 16)
            sp.wait_ge(setup, 100)
            sp.dma_start(wsum_d.rearrange("(b p e) o -> p b (e o)", p=P, e=TILE), S_t).then_inc(maskst, 16)

            def prefetch(h, chunk, mask):
                sp.dma_start(mring[:, h, :], mask[bass.ds(chunk * CE, CE)].partition_broadcast(P)).then_inc(mld[h], 16)

            def edge_pass(p, mask, src_ev, src_scan, K=1, D=0):
                if p == 0:
                    sp.wait_ge(maskst, 48)
                for h in range(R):
                    if p > 0:
                        sp.wait_ge(mld[h], 16 * 50 * p)
                    prefetch(h, h, mask)

                def body(i, first):
                    for h in range(R):
                        c = i * R + h
                        src_ev(c)
                        sp.dma_start(run_d[bass.ds(c * CE, CE), :].rearrange("(k e) f -> e k f", e=TILE),
                                     OS[:, h % 2, :].rearrange("e (k f) -> e k f", f=F)).then_inc(odma[h % 2], 16)
                        src_scan(c)
                        prefetch(h, c + R, mask)
                fori(sp, p, body)

            for r in range(2):
                sp.wait_ge(h_ready, r + 1)
                sp.dma_start(tabs[r].rearrange("(j p) f -> p j f", p=P), H[:, :, :]).then_inc(tabst, 16)
                edge_pass(r, keep_d, lambda c: sp.wait_ge(ev, r * NC + c + 1), lambda c: sp.wait_ge(scan, r * NC + c + 1))
            sp.wait_ge(mev, MEV_L1)
            sp.dma_start(tabs[2].rearrange("(j p) f -> p j f", p=P), V[:, :, :]).then_inc(tabst, 16)
            edge_pass(2, keep_d, lambda c: sp.wait_ge(ev, 2 * NC + c + 1), lambda c: sp.wait_ge(scan, 2 * NC + c + 1))
            for g in range(NG):
                sp.wait_ge(mev, MEV_L2 + g + 1)
                sp.dma_start(tab_sv[g * 512:(g + 1) * 512, :].rearrange("(k p) f -> p k f", p=P), EV[:, g % 2, :, 0:256]).then_inc(attst[g % 2], 16)
                sp.dma_start(tab_d[g * 512:(g + 1) * 512, :].rearrange("(k p) f -> p k f", p=P), EV[:, g % 2, :, 256:384]).then_inc(attst[g % 2], 16)
            edge_pass(3, cut_d, lambda c: sp.wait_ge(ev, 3 * NC + c + 1), lambda c: sp.wait_ge(gchain, GK * c + GD1))
            sp.wait_ge(tre, TRE_H1N)
            sp.dma_start(tabs[3].rearrange("(j p) f -> p j f", p=P), V[:, :, :]).then_inc(tabst, 16)
            edge_pass(4, keep_d, lambda c: sp.wait_ge(ev, 4 * NC + c + 1), lambda c: sp.wait_ge(scan, 3 * NC + c + 1))
            for h in range(R):
                sp.wait_ge(mld[h], 16 * 250)
            sp.wait_ge(osem, 1)
            sp.dma_start(out[0:(NBR - 1) * P, :].rearrange("(j p) f -> p j f", p=P), X[:, 0:NBR - 1, :]).then_inc(zsem, 16)
            sp.dma_start(out[(NBR - 1) * P:N, :], X[0:TAIL, NBR - 1, :]).then_inc(zsem, 16)
            sp.wait_ge(zsem, 32)

        @block.gpsimd
        def _(pool):
            pool.memset(ident[:, :], 0.0).then_inc(cst, 1)
            pool.memset(ones[:, :], 1.0).then_inc(cst, 1)
            pool.iota(nval_i[:, :], pattern=[[P, NB]], base=0, channel_multiplier=1).then_inc(cst, 1)
            pool.wait_ge(cst, 1)
            pool.affine_select(out=ident[:, :], in_=ident[:, :], compare_op=ALU.not_equal, fill=1.0, base=0,
                               pattern=[[-1, P]], channel_multiplier=1).then_inc(cst, 1)

            def rows_of(dest, table, idx, done):
                pool.indirect_dma_start(dest, None, table, bass.IndirectOffsetOnAxis(ap=idx, axis=0)).then_inc(done, 16)

            pool.wait_ge(dpad, 32)
            pool.wait_ge(setup, 7)
            for j in range(NB):
                rows_of(rows_i[:, j, :], dst_rows, trow_i[:, j:j + 1], rowg)
            pool.wait_ge(setup, 102)
            pool.wait_ge(maskst, 48)
            for j in range(NB):
                rows_of(wlast[:, j:j + 1], wsum_d, last_i[:, j:j + 1], wg)

            def sum_pass(s, ntab):
                pool.wait_ge(tabst, ntab)

                def body(i, first):
                    for h in range(R):
                        pool.wait_ge(staged, s * (NC + R) + i * R + h + 1)
                        pool.sem_inc(turn, 1)
                        for k in range(CT):
                            rows_of(G[:, h, k, 0:F], tabs[s], stage[:, h, 0, k:k + 1], gath[h])
                fori(pool, s, body)

            def att_pass():
                for q in range(2):
                    pool.wait_ge(attst[q], 32 * ((NG + 1 - q) // 2))

                def body(i, first):
                    for h in range(R):
                        pool.wait_ge(gstaged, i * R + h + 1)
                        pool.sem_inc(turn, 1)
                        for k in range(CT):
                            rows_of(G[:, h, k, 0:2 * F], tab_sv, stage[:, h, 0, k:k + 1], ggath[h])
                            rows_of(G[:, h, k, 2 * F:3 * F], tab_d, stage[:, h, 1, k:k + 1], ggath[h])
                fori(pool, 1, body)

            def node_rows(p):
                for q in range(2):
                    pool.wait_ge(odma[q], 16 * (NC // 2) * (p + 1))
                for j in range(NBR):
                    rows_of(A[:, j, :], run_d, last_i[:, j:j + 1], agg)

            sum_pass(0, 16)
            node_rows(0)
            sum_pass(1, 32)
            node_rows(1)
            sum_pass(2, 48)
            node_rows(2)
            att_pass()
            node_rows(3)
            sum_pass(3, 64)
            node_rows(4)

        @block.tensor
        def _(pe):
            def turn4(bank, blocks):
                for k, b in enumerate(blocks):
                    last = nc.tensor.transpose(PS[:, bank, k * P:(k + 1) * P], b, ident[:, :])
                return last

            state = {"tr": 0}

            def turn_nodes(src, first_of=lambda g: None):
                for g in range(NG):
                    first_of(g)
                    n = state["tr"]
                    if n >= 2:
                        pe.wait_ge(tre, n - 1)
                    turn4(4 + n % 2, [src(4 * g + k) for k in range(4)]).then_inc(tr, 1)
                    state["tr"] += 1

            pe.wait_ge(cst, 4)
            pe.wait_ge(ldw, 16 * 27)
            for g in range(8):
                n = state["tr"]
                if n >= 2:
                    pe.wait_ge(tre, n - 1)
                turn4(4 + n % 2, [WN[:, b, :] for b in range(4 * g, min(4 * g + 4, NWB))]).then_inc(tr, 1)
                state["tr"] += 1
            for n, (tab, need) in enumerate(((src_f, 1), (dclip, 2), (w_t, 2))):
                pe.wait_ge(setup, need)
                if n == 2:
                    pe.wait_ge(pst, 1)
                    pe.wait_ge(setup, 4)
                    pe.wait_ge(ld, 16 * 11)
                b0 = 2 * (n % 2)
                for b in range(EB):
                    last = nc.tensor.transpose(PS[:, b0 + b // 4, (b % 4) * P:(b % 4 + 1) * P], tab[:, b, :], ident[:, :])
                last.then_inc(pst, 1)
            pe.wait_ge(setup, 6)
            for b in range(EB):
                last = nc.tensor.matmul(PS[:, 2 + b // 4, (b % 4) * P:(b % 4 + 1) * P], fbc[:, b, :], ident[:, :], start=True, stop=True)
            last.then_inc(pst, 1)
            pe.wait_ge(setup, 50)
            for u, t in enumerate((P_t, lead)):
                for b in range(EB):
                    last = nc.tensor.matmul(PS[0:1, 6 + b // 4, (b % 4) * P:(b % 4 + 1) * P] if u == 0 else PS[0:1, b // 4, (b % 4) * P:(b % 4 + 1) * P],
                                            t[:, b, P - 1:P], ident[:, :], start=True, stop=True)
            last.then_inc(pst, 1)
            pe.wait_ge(setup, 51)
            for b in range(EB):
                last = nc.tensor.matmul(PS[:, 6, b:b + 1], carry[0:1, b * P:(b + 1) * P], ones[0:1, 0:1], start=True, stop=True)
            last.then_inc(pst, 1)
            pe.wait_ge(setup, 101)
            pe.wait_ge(tre, 8)
            for j in range(NB):
                last = nc.tensor.matmul(PS[0:1, j // 4, (j % 4) * P:(j % 4 + 1) * P], cum[:, j:j + 1], ident[:, :], start=True, stop=True)
            last.then_inc(pst, 1)
            pe.wait_ge(setup, 103)
            for j in range(NB):
                last = nc.tensor.matmul(PS[:, 7, j:j + 1], degrow[0:1, j * P:(j + 1) * P], ones[0:1, 0:1], start=True, stop=True)
            last.then_inc(pst, 1)
            pe.wait_ge(setup, 104)

            def sum_pass(s, p, weighted):
                C = s * NC
                CA = p * NC

                def body(i, first):
                    for h in range(R):
                        c, q = i * R + h, h % 2
                        if weighted:
                            pe.wait_ge(scaled, c + 1)
                        else:
                            pe.wait_ge(gath[h], 64 * (s * IT + i) + 64)
                        if not (first and h < 2):
                            pe.wait_ge(scan, C + c - 1)
                        turn4(q, [G[:, h, k, 0:F] for k in range(CT)]).then_inc(xt, 1)
                        pe.wait_ge(scan, C + c + 1)
                        if not (first and h < 2):
                            pe.wait_ge(ev, CA + c - 1)
                        turn4(2 + q, [ST[:, q, k * P:(k + 1) * P] for k in range(CT)]).then_inc(back, 1)
                fori(pe, s, body)

            def att_pass():
                def body(i, first):
                    for h in range(R):
                        c, q = i * R + h, h % 2
                        pe.wait_ge(ggath[h], 128 * i + 128)
                        if not (first and h < 2):
                            pe.wait_ge(gchain, GK * (c - 2) + GNV)
                        for k in range(CT):
                            o = PS[:, q, k * P:(k + 1) * P]
                            nc.tensor.matmul(o, G[:, h, k, 0:F], ident[:, :], start=True, stop=False)
                            nc.tensor.matmul(o, G[:, h, k, 2 * F:3 * F], ident[:, :], start=False, stop=True)
                        turn4(6 + q, [G[:, h, k, F:2 * F] for k in range(CT)]).then_inc(ga, 1)
                        pe.wait_ge(gchain, GK * c + GQ)
                        if not (first and h < 2):
                            pe.wait_ge(ev, 3 * NC + c - 1)
                        turn4(2 + q, [NN[:, q, k * P:(k + 1) * P] for k in range(CT)]).then_inc(back, 1)
                body(0, True)
                with pe.Fori(1, IT) as i:
                    body(i, False)

            st = {"mm": 0, "gr": 0}
            for r in range(2):
                o = r * 13
                pe.wait_ge(h_ready, r + 1)
                turn_nodes(lambda b: H[:, b, :])
                pe.wait_ge(v_ready, r + 1)
                turn_nodes(lambda b: V[:, b, :])
                sum_pass(r, r, False)
                pe.wait_ge(a_ready, r + 1)
                turn_nodes(lambda b: A[:, b, :])
                pe.wait_ge(tre, state["tr"])
                for g in range(NG):
                    n = slice(g * 512, (g + 1) * 512)
                    if st["mm"]:
                        pe.wait_ge(mev, st["mm"])
                    for m in range(2):
                        nc.tensor.matmul(PS[:, 6 + m, :], WT[:, o + 2 * m, :], AT[:, n], start=True, stop=False)
                        nc.tensor.matmul(PS[:, 6 + m, :], WT[:, o + 2 * m + 1, :], VT[:, n], start=False, stop=False)
                        last = nc.tensor.matmul(PS[:, 6 + m, :], brow[0:1, BM(r) + m * P:BM(r) + (m + 1) * P], degrow[0:1, n], start=False, stop=True)
                    last.then_inc(mm, 1)
                    st["mm"] += 1
                    pe.wait_ge(mev, st["mm"])
                    if st["gr"]:
                        pe.wait_ge(gdve, 2 * st["gr"] - 1)
                    ih = WT[:, o + 4:o + 10, :].rearrange("p (q m) c -> p q m c", m=2)
                    hh = WT[:, o + 10:o + 13, :]
                    for k in range(4):
                        on = ones[0:1, :]
                        hb = HT[:, g * 512 + k * P:g * 512 + (k + 1) * P]
                        m0, m1 = (M2[:, g % 2, m, k * P:(k + 1) * P] for m in range(2))
                        rz, inn, hn = PS[:, k, 0:256], PS[:, k, 256:384], PS[:, k, 384:512]
                        nc.tensor.matmul(rz, m0, ih[:, 0:2, 0, :], start=True, stop=False)
                        nc.tensor.matmul(rz, m1, ih[:, 0:2, 1, :], start=False, stop=False)
                        nc.tensor.matmul(rz, hb, hh[:, 0:2, :], start=False, stop=False)
                        nc.tensor.matmul(rz, on, brow[0:1, BI(r):BI(r) + 256], start=False, stop=False)
                        nc.tensor.matmul(rz, on, brow[0:1, BH(r):BH(r) + 256], start=False, stop=True)
                        nc.tensor.matmul(inn, m0, ih[:, 2, 0, :], start=True, stop=False)
                        nc.tensor.matmul(inn, m1, ih[:, 2, 1, :], start=False, stop=False)
                        nc.tensor.matmul(inn, on, brow[0:1, BI(r) + 256:BI(r) + 384], start=False, stop=True)
                        nc.tensor.matmul(hn, hb, hh[:, 2, :], start=True, stop=False)
                        last = nc.tensor.matmul(hn, on, brow[0:1, BH(r) + 256:BH(r) + 384], start=False, stop=True)
                    last.then_inc(gr, 1)
                    st["gr"] += 1
            pe.wait_ge(h_ready, 3)
            turn_nodes(lambda b: H[:, b, :])
            pe.wait_ge(tre, state["tr"])

            def product(groups, banks, lag):
                for g in range(NG):
                    if st["mm"]:
                        pe.wait_ge(mev, st["mm"] - lag)
                    groups(g).then_inc(mm, 1)
                    st["mm"] += 1

            def xw(g):
                for k in range(4):
                    last = nc.tensor.matmul(PS[:, 6 + g % 2, k * P:(k + 1) * P], HT[:, g * 512 + k * P:g * 512 + (k + 1) * P], WD[:, 0, :], start=True, stop=True)
                return last
            product(xw, None, 0)
            sum_pass(2, 2, True)
            pe.wait_ge(h_ready, 4)
            turn_nodes(lambda b: H[:, b, :])
            pe.wait_ge(tre, state["tr"])

            def qkv(g):
                for k in range(4):
                    nc.tensor.matmul(PS[:, k, 0:384], HT[:, g * 512 + k * P:g * 512 + (k + 1) * P], WT[:, 26:29, :], start=True, stop=False)
                    last = nc.tensor.matmul(PS[:, k, 0:384], ones[0:1, :], brow[0:1, BQ:BQ + 384], start=False, stop=True)
                return last
            product(qkv, None, 0)
            pe.wait_ge(mev, st["mm"])
            att_pass()
            pe.wait_ge(h_ready, 5)
            turn_nodes(lambda b: H[:, b, :])
            pe.wait_ge(tre, state["tr"])
            product(lambda g: nc.tensor.matmul(PS[:, 6 + g % 2, :], WD[:, 1, :], HT[:, g * 512:(g + 1) * 512], start=True, stop=True), None, 0)
            pe.wait_ge(mev, st["mm"])
            turn_nodes(lambda b: VT[:, b * P:(b + 1) * P])
            assert state["tr"] == TRE_H1N
            sum_pass(3, 4, False)
            pe.wait_ge(a_ready, 3)
            turn_nodes(lambda b: A[:, b, :])
            pe.wait_ge(tre, state["tr"])

            def hidden(g):
                nc.tensor.matmul(PS[:, 6 + g % 2, :], WD[:, 2, :], VT[:, g * 512:(g + 1) * 512], start=True, stop=False)
                return nc.tensor.matmul(PS[:, 6 + g % 2, :], WD[:, 3, :], AT[:, g * 512:(g + 1) * 512], start=False, stop=True)
            product(hidden, None, 0)
            pe.wait_ge(mev, st["mm"])

            def last_product(g):
                for k in range(4):
                    nc.tensor.matmul(PS[:, 6 + g % 2, k * P:(k + 1) * P], HT[:, g * 512 + k * P:g * 512 + (k + 1) * P], WD[:, 4, :], start=True, stop=False)
                    last = nc.tensor.matmul(PS[:, 6 + g % 2, k * P:(k + 1) * P], ones[0:1, :], brow[0:1, B2:B2 + P], start=False, stop=True)
                return last
            product(last_product, None, 0)

        @block.scalar
        def _(act):
            state = {"tr": 0, "mm": 0, "gr": 0}

            def take(dests):
                for d in dests:
                    n = state["tr"]
                    act.wait_ge(tr, n + 1)
                    nc.scalar.activation(d, PS[:, 4 + n % 2, 0:d.free_size()], ACT.Copy).then_inc(tre, 1)
                    state["tr"] += 1

            def groups(t):
                return [t[:, g * 512:(g + 1) * 512] for g in range(NG)]

            wt = WT[:, :, :].rearrange("p b c -> p (b c)")
            take([wt[:, g * 512:min((g + 1) * 512, NWB * P)] for g in range(8)])
            act.wait_ge(setup, 105)
            nc.scalar.activation(dis[:, :], tmpn[:, :], ACT.Sqrt).then_inc(sq, 1)

            def ln_sqrt(n):
                act.wait_ge(lnv, n)
                nc.scalar.activation(rstd[:, 0:NBR], tmpn[:, 0:NBR], ACT.Sqrt).then_inc(lns, 1)

            def sum_pass(s, p, weighted):
                CA = p * NC

                def body(i, first):
                    for h in range(R):
                        c, q = i * R + h, h % 2
                        if weighted:
                            act.wait_ge(gath[h], 64 * (s * IT + i) + 64)
                            act.sem_inc(turn, 1)
                            for k in range(CT):
                                last = nc.scalar.activation(G[:, h, k, 0:F], G[:, h, k, 0:F], ACT.Copy, scale=w_e[:, bass.ds(c * CT + k, 1)])
                            last.then_inc(scaled, 1)
                        act.wait_ge(back, CA + c + 1)
                        if not (first and h < 2):
                            act.wait_ge(odma[q], 16 * (p * (NC // 2) + i * 2 + h // 2))
                        nc.scalar.activation(OS[:, q, :], PS[:, 2 + q, :], ACT.Copy).then_inc(ev, 1)
                fori(act, s, body)

            def att_pass():
                def body(i, first):
                    for h in range(R):
                        c, q = i * R + h, h % 2
                        act.wait_ge(ga, c + 1)
                        if not (first and h < 2):
                            act.wait_ge(gchain, GK * (c - 2) + GD1)
                        nc.scalar.activation(Ee[:, q, :], PS[:, q, :], ACT.Copy, scale=0.2).then_inc(ge, 1)
                        act.wait_ge(gchain, GK * c + GD1)
                        nc.scalar.activation(D01[:, q, :], D01[:, q, :], ACT.Exp).then_inc(gx, 1)
                        act.wait_ge(back, 3 * NC + c + 1)
                        act.wait_ge(odma[q], 16 * (3 * (NC // 2) + i * 2 + h // 2))
                        nc.scalar.activation(OS[:, q, :], PS[:, 2 + q, :], ACT.Copy).then_inc(ev, 1)
                body(0, True)
                with act.Fori(1, IT) as i:
                    body(i, False)

            ln_sqrt(1)
            for r in range(2):
                take(groups(HT))
                take(groups(VT))
                sum_pass(r, r, False)
                take(groups(AT))
                for g in range(NG):
                    act.wait_ge(mm, state["mm"] + 1)
                    if state["gr"] >= 2:
                        act.wait_ge(gr, state["gr"] - 1)
                    nc.scalar.activation(M2[:, g % 2, :, :], PS[:, 6:8, :], ACT.Copy).then_inc(mev, 1)
                    state["mm"] += 1
                    state["gr"] += 1
                    act.wait_ge(gr, state["gr"])
                    if state["gr"] > 1:
                        act.wait_ge(gdve, 2 * (state["gr"] - 1))
                    nc.scalar.activation(rgate.rearrange("p (k c) -> p k c", c=P), PS[:, 0:4, 0:128], ACT.Sigmoid)
                    nc.scalar.activation(omz.rearrange("p (k c) -> p k c", c=P), PS[:, 0:4, 128:256], ACT.Sigmoid, scale=-1.0).then_inc(gact, 1)
                    act.wait_ge(gdve, 2 * state["gr"] - 1)
                    nc.scalar.activation(tnh, cand, ACT.Tanh).then_inc(gact, 1)
            ln_sqrt(2)
            take(groups(HT))
            for g in range(NG):
                act.wait_ge(mm, state["mm"] + 1)
                for k in range(4):
                    last = nc.scalar.activation(V[:, 4 * g + k, :], PS[:, 6 + g % 2, k * P:(k + 1) * P], ACT.Copy, scale=dis[:, 4 * g + k:4 * g + k + 1])
                last.then_inc(mev, 1)
                state["mm"] += 1
            assert state["mm"] == MEV_L1
            sum_pass(2, 2, True)
            ln_sqrt(3)
            take(groups(HT))
            for g in range(NG):
                act.wait_ge(mm, state["mm"] + 1)
                if g >= 2:
                    act.wait_ge(attst[g % 2], 32 * (g // 2))
                nc.scalar.activation(EV[:, g % 2, :, :], PS[:, 0:4, 0:384], ACT.Copy).then_inc(mev, 1)
                state["mm"] += 1
            att_pass()
            ln_sqrt(4)
            take(groups(HT))
            for g in range(NG):
                act.wait_ge(mm, state["mm"] + 1)
                nc.scalar.activation(VT[:, g * 512:(g + 1) * 512], PS[:, 6 + g % 2, :], ACT.Relu, bias=bcol[:, 0:1]).then_inc(mev, 1)
                state["mm"] += 1
            take([V[:, 4 * g:4 * g + 4, :] for g in range(NG)])
            sum_pass(3, 4, False)
            take(groups(AT))
            for g in range(NG):
                act.wait_ge(mm, state["mm"] + 1)
                nc.scalar.activation(HT[:, g * 512:(g + 1) * 512], PS[:, 6 + g % 2, :], ACT.Relu, bias=bcol[:, 1:2]).then_inc(mev, 1)
                state["mm"] += 1
            for g in range(NG):
                act.wait_ge(mm, state["mm"] + 1)
                nc.scalar.activation(H[:, 4 * g:4 * g + 4, :].rearrange("p k c -> p (k c)"), PS[:, 6 + g % 2, :], ACT.Relu).then_inc(mev, 1)
                state["mm"] += 1

        @block.vector
        def _(dve):
            chain = {"n": 0}

            def step(ins):
                chain["n"] += 1
                ins.then_inc(nstep, 1)
                dve.wait_ge(nstep, chain["n"])

            v = nc.vector
            v.memset(dst_i[:, :, :], NONE)
            v.memset(src_i[:, :, :], 0)
            v.memset(noprev[:, :], -1)
            v.memset(w_t[:, :, :], 0.0).then_inc(cleared, 2)
            step(v.memset(H[:, NBR:NB, :], 0.0))
            v.memset(X[:, NBR - 1:NB, :], 0.0).then_inc(cleared, 2)
            step(v.memset(carry[:, 0:1], 0.0))
            step(v.memset(zero[:, :], 0.0))
            step(v.memset(ST[:, :, :], 0.0))
            step(v.memset(RB[:, :, :], 0.0))
            step(v.memset(DN[:, :, :], 0.0))
            step(v.memset(NN[:, :, :], 0.0))
            dve.wait_ge(cleared, 4)
            dve.wait_ge(ld, 16 * 11)
            v.tensor_copy(src_f, src_i[:, :, :]).then_inc(setup, 1)
            step(v.tensor_copy(dst_f[:, :, :], dst_i[:, :, :]))
            v.tensor_scalar(dclip, dst_f[:, :, :], float(NB * P - 1), None, ALU.min).then_inc(setup, 1)
            dve.wait_ge(cst, 4)
            dve.wait_ge(pst, 1)
            pv = PS[:, :, :].rearrange("p b c -> p (b c)")
            v.tensor_copy(src_e[:, :], pv[:, 0:TR]).then_inc(setup, 1)
            dve.wait_ge(pst, 2)
            v.tensor_copy(dst_e[:, :], pv[:, 1024:1024 + TR]).then_inc(setup, 1)
            dve.wait_ge(prevld, 16)
            step(v.tensor_copy(prev_f[:, :], prev_i[:, :]))
            v.tensor_tensor(keep_t[:, :, 1:TILE], dst_f[:, :, 1:TILE], dst_f[:, :, 0:TILE - 1], ALU.is_equal)
            step(v.tensor_tensor(keep_t[:, :, 0], dst_f[:, :, 0], prev_f[:, :], ALU.is_equal))
            v.tensor_scalar(cut_t[:, :, :], keep_t[:, :, :], BIG, -BIG, ALU.mult, ALU.add).then_inc(setup, 1)
            v.tensor_copy(fbc, dst_f[:, :, 0:1].to_broadcast([P, EB, P])).then_inc(setup, 1)
            step(v.tensor_copy(nval[:, :], nval_i[:, :]))
            dve.wait_ge(pst, 3)
            step(v.tensor_copy(w_e[:, :], pv[:, 0:TR]))
            dve.wait_ge(pst, 4)
            for j in range(NB):
                step(v.tensor_scalar(junk, pv[:, 1024:1024 + TR], nval[:, j:j + 1], 0.0, ALU.is_le, ALU.add, accum_out=cnt[:, j:j + 1]))
            step(v.tensor_scalar(trow[:, :], cnt[:, :], 1.0, 1.0, ALU.max, ALU.mult))
            v.tensor_copy(trow_i[:, :], trow[:, :]).then_inc(setup, 1)
            for b in range(EB):
                v.tensor_tensor_scan(P_t[:, b, :], keep_t[:, b, :], w_t[:, b, :], 0.0, ALU.mult, ALU.add)
                last = v.tensor_tensor_scan(lead[:, b, :], keep_t[:, b, :], zero[:, :], 1.0, ALU.mult, ALU.add)
            last.then_inc(setup, 43)
            dve.wait_ge(pst, 5)
            v.tensor_copy(tails[:, 0, :], pv[0:1, 3072:3072 + TR])
            step(v.tensor_copy(tails[:, 1, :], pv[0:1, 0:TR]))
            v.tensor_tensor_scan(carry[:, 1:TR + 1], tails[:, 1, :], tails[:, 0, :], 0.0, ALU.mult, ALU.add).then_inc(setup, 1)
            dve.wait_ge(pst, 6)
            step(v.tensor_copy(cprev[:, :], PS[:, 6, 0:EB]))
            for b in range(EB):
                last = v.scalar_tensor_tensor(S_t[:, b, :], lead[:, b, :], cprev[:, b:b + 1], P_t[:, b, :], ALU.mult, ALU.add)
            last.then_inc(setup, 49)
            dve.wait_ge(rowg, 16 * NB)
            for j in range(NB):
                step(v.tensor_scalar(junk[:, 0:TILE], rows_i[:, j, :], nval[:, j:j + 1], 0.0, ALU.is_le, ALU.add, accum_out=cnt2[:, j:j + 1]))
            step(v.tensor_scalar(trow[:, :], trow[:, :], -1.0, float(TILE), ALU.add, ALU.mult))
            v.tensor_tensor(cum[:, :], trow[:, :], cnt2[:, :], ALU.add).then_inc(setup, 1)
            dve.wait_ge(setup, 101)
            step(v.tensor_scalar(trow[:, :], cum[:, :], -1.0, 0.0, ALU.add, ALU.max))
            v.tensor_copy(last_i[:, :], trow[:, :]).then_inc(setup, 1)
            dve.wait_ge(pst, 7)
            step(v.memset(row[:, 0:1], 0.0))
            step(v.tensor_copy(row[:, 1:NB * P + 1], pv[0:1, 0:NB * P]))
            v.tensor_tensor(degrow[:, :], row[:, 1:NB * P + 1], row[:, 0:NB * P], ALU.subtract).then_inc(setup, 1)
            dve.wait_ge(pst, 8)
            v.tensor_copy(deg[:, :], PS[:, 7, 0:NB]).then_inc(setup, 1)
            dve.wait_ge(setup, 104)
            step(v.tensor_scalar(has[:, :], deg[:, :], 1.0, None, ALU.min))
            step(v.tensor_scalar(invdeg[:, :], deg[:, :], 1.0, None, ALU.max))
            step(v.reciprocal(invdeg[:, :], invdeg[:, :]))
            step(v.tensor_tensor(invdeg[:, :], invdeg[:, :], has[:, :], ALU.mult))
            dve.wait_ge(wg, 16 * NB)
            step(v.tensor_tensor(wlast[:, :], wlast[:, :], has[:, :], ALU.mult))
            step(v.tensor_scalar(wlast[:, :], wlast[:, :], 1.0, None, ALU.add))
            step(v.tensor_scalar(tmpn[:, :], wlast[:, :], 1e-30, None, ALU.max))
            v.reciprocal(tmpn[:, :], tmpn[:, :]).then_inc(setup, 1)
            step(v.tensor_scalar(wlast[:, :], wlast[:, :], 0.0, None, ALU.is_gt))
            dve.wait_ge(sq, 1)
            step(v.tensor_tensor(dis[:, :], dis[:, :], wlast[:, :], ALU.mult))

            def bc(t):
                return t[:, 0:NBR].unsqueeze(2).to_broadcast([P, NBR, F])

            def bcn(t):
                return t[:, :].unsqueeze(2).to_broadcast([P, NB, F])

            def layernorm(n):
                x, c, h = X[:, 0:NBR, :], A[:, 0:NBR, :], H[:, 0:NBR, :]
                step(v.tensor_reduce(mean[:, 0:NBR], x, AX.X, ALU.add))
                step(v.tensor_scalar(mean[:, 0:NBR], mean[:, 0:NBR], 1.0 / F, None, ALU.mult))
                step(v.tensor_tensor(c, x, bc(mean), ALU.subtract))
                step(v.tensor_tensor(h, c, c, ALU.mult))
                step(v.tensor_reduce(tmpn[:, 0:NBR], h, AX.X, ALU.add))
                v.tensor_scalar(tmpn[:, 0:NBR], tmpn[:, 0:NBR], 1.0 / F, EPS, ALU.mult, ALU.add).then_inc(lnv, 1)
                dve.wait_ge(lns, n)
                step(v.reciprocal(rstd[:, 0:NBR], rstd[:, 0:NBR]))
                v.scalar_tensor_tensor(h, c, 0.0, bc(rstd), ALU.max, ALU.mult).then_inc(h_ready, 1)

            def stage_ahead(h, tile, done):
                v.tensor_scalar(stage[:, h, 0, :], src_e[:, bass.ds(tile, CT)], 0.0, None, ALU.add).then_inc(done, 1)

            def sum_pass(s, p):
                C = s * NC
                if s:
                    dve.wait_ge(staged, s * (NC + R))
                for h in range(R):
                    stage_ahead(h, h * CT, staged)

                def body(i, first):
                    for h in range(R):
                        c, q = i * R + h, h % 2
                        dve.wait_ge(mld[h], 16 * (50 * p + i) + 16)
                        dve.wait_ge(xt, C + c + 1)
                        if not (first and h < 2):
                            dve.wait_ge(back, p * NC + c - 1)
                        if not (first and h < 1):
                            dve.wait_ge(scan, C + c)
                        v.tensor_tensor_scan(ST[:, q, :], mring[:, h, :], PS[:, q, :], ST[:, 1 - q, CE - 1:CE], ALU.mult, ALU.add).then_inc(scan, 1)
                        stage_ahead(h, (c + R) * CT, staged)
                fori(dve, s, body)

            def att_pass():
                def stage_both(h, tile):
                    v.tensor_scalar(stage[:, h, 0, :], src_e[:, bass.ds(tile, CT)], 0.0, None, ALU.add)
                    v.tensor_scalar(stage[:, h, 1, :], dst_e[:, bass.ds(tile, CT)], 0.0, None, ALU.add).then_inc(gstaged, 1)
                dve.wait_ge(staged, 3 * (NC + R))
                for h in range(R):
                    stage_both(h, h * CT)

                def body(i, first):
                    for h in range(R):
                        c, q = i * R + h, h % 2

                        def done(ins, n, wait=True):
                            ins.then_inc(gchain, 1)
                            if wait:
                                dve.wait_ge(gchain, GK * c + n)
                        dve.wait_ge(mld[h], 16 * (50 * 3 + i) + 16)
                        dve.wait_ge(ge, c + 1)
                        done(v.tensor_tensor(Ee[:, q, :], PS[:, q, :], Ee[:, q, :], ALU.max), 1, False)
                        done(v.tensor_copy(RB[:, q, 0:1], RB[:, 1 - q, CE:CE + 1]), 2)
                        done(v.tensor_tensor_scan(RB[:, q, 1:CE + 1], mring[:, h, :], Ee[:, q, :], RB[:, q, 0:1], ALU.add, ALU.max), 3)
                        done(v.tensor_tensor(D01[:, q, 0:CE], RB[:, q, 0:CE], mring[:, h, :], ALU.add), 4)
                        done(v.tensor_tensor(D01[:, q, 0:CE], D01[:, q, 0:CE], RB[:, q, 1:CE + 1], ALU.subtract), 5, False)
                        done(v.tensor_tensor(D01[:, q, CE:2 * CE], Ee[:, q, :], RB[:, q, 1:CE + 1], ALU.subtract), GD1, False)
                        stage_both(h, (c + R) * CT)
                        dve.wait_ge(gx, c + 1)
                        done(v.tensor_tensor(NV[:, q, :], D01[:, q, CE:2 * CE], PS[:, 6 + q, :], ALU.mult), GNV)
                        done(v.tensor_tensor_scan(DN[:, q, :], D01[:, q, 0:CE], D01[:, q, CE:2 * CE], DN[:, 1 - q, CE - 1:CE], ALU.mult, ALU.add), 8)
                        if not (first and h < 2):
                            dve.wait_ge(back, 3 * NC + c - 1)
                        done(v.tensor_tensor_scan(ST[:, q, :], D01[:, q, 0:CE], NV[:, q, :], ST[:, 1 - q, CE - 1:CE], ALU.mult, ALU.add), 9, False)
                        done(v.reciprocal(D01[:, q, CE:2 * CE], DN[:, q, :]), 10)
                        done(v.tensor_tensor(NN[:, q, :], ST[:, q, :], D01[:, q, CE:2 * CE], ALU.mult), GQ, False)
                body(0, True)
                with dve.Fori(1, IT) as i:
                    body(i, False)

            layernorm(1)
            st = {"gr": 0}
            for r in range(2):
                dve.wait_ge(h_ready, r + 1)
                if r == 0:
                    dve.wait_ge(maskst, 48)
                    dve.wait_ge(wg, 16 * NB)
                else:
                    dve.wait_ge(tre, 8 + 3 * NG)
                v.tensor_tensor(V[:, :, :], H[:, :, :], bcn(deg), ALU.mult).then_inc(v_ready, 1)
                if r == 0:
                    step(v.memset(A[:, NBR:NB, :], 0.0))
                sum_pass(r, r)
                dve.wait_ge(agg, 16 * NBR * (r + 1))
                v.tensor_tensor(A[:, 0:NBR, :], A[:, 0:NBR, :], bc(has), ALU.mult).then_inc(a_ready, 1)
                dve.wait_ge(tabst, 16 * (r + 1))
                for g in range(NG):
                    n = st["gr"]
                    kk = slice(4 * g, 4 * g + 4)
                    dve.wait_ge(gact, 2 * n + 1)
                    cd = cand.rearrange("p (k c) -> p k c", c=P)
                    tn = tnh.rearrange("p (k c) -> p k c", c=P)
                    oz = omz.rearrange("p (k c) -> p k c", c=P)
                    step(v.tensor_tensor(cd, rgate.rearrange("p (k c) -> p k c", c=P), PS[:, 0:4, 384:512], ALU.mult))
                    v.tensor_tensor(cd, cd, PS[:, 0:4, 256:384], ALU.add).then_inc(gdve, 1)
                    dve.wait_ge(gact, 2 * n + 2)
                    step(v.tensor_tensor(tn, tn, H[:, kk, :], ALU.subtract))
                    step(v.tensor_tensor(tn, tn, oz, ALU.mult))
                    step(v.tensor_tensor(tn, tn, has[:, kk].unsqueeze(2).to_broadcast([P, 4, F]), ALU.mult))
                    v.tensor_tensor(H[:, kk, :], H[:, kk, :], tn, ALU.add).then_inc(gdve, 1)
                    st["gr"] += 1
                dve.wait_ge(gdve, 2 * st["gr"])
                if r == 0:
                    dve.sem_inc(h_ready, 1)
            step(v.tensor_tensor(X[:, 0:NBR, :], X[:, 0:NBR, :], H[:, 0:NBR, :], ALU.add))
            layernorm(2)
            dve.wait_ge(h_ready, 3)

            sum_pass(2, 2)
            dve.wait_ge(agg, 16 * NBR * 3)
            dve.wait_ge(tabst, 48)
            r_ = slice(0, NBR)
            step(v.tensor_tensor(A[:, r_, :], A[:, r_, :], bc(has), ALU.mult))
            step(v.tensor_tensor(A[:, r_, :], A[:, r_, :], V[:, r_, :], ALU.add))
            step(v.tensor_tensor(A[:, r_, :], A[:, r_, :], bc(dis), ALU.mult))
            step(v.tensor_tensor(A[:, r_, :], A[:, r_, :], b1bc[:, :].unsqueeze(1).to_broadcast([P, NBR, F]), ALU.add))
            step(v.tensor_tensor(X[:, r_, :], X[:, r_, :], A[:, r_, :], ALU.add))
            layernorm(3)
            dve.wait_ge(h_ready, 4)

            att_pass()
            dve.wait_ge(agg, 16 * NBR * 4)
            step(v.tensor_tensor(A[:, r_, :], A[:, r_, :], bc(has), ALU.mult))
            step(v.tensor_tensor(X[:, r_, :], X[:, r_, :], A[:, r_, :], ALU.add))
            layernorm(4)
            dve.wait_ge(h_ready, 5)

            sum_pass(3, 4)
            dve.wait_ge(agg, 16 * NBR * 5)
            v.tensor_tensor(A[:, r_, :], A[:, r_, :], bc(invdeg), ALU.mult).then_inc(a_ready, 1)
            dve.wait_ge(mev, MEV_L1 + 4 * NG)
            v.tensor_tensor(X[:, r_, :], X[:, r_, :], H[:, r_, :], ALU.add).then_inc(osem, 1)


MEV_L1 = 3 * NG
MEV_L2 = 3 * NG
TRE_H1N = 8 + 10 * NG
GK, GD1, GNV, GQ = 11, 6, 7, 11


_INS = ["x", "src", "dst", "edge_weight", "L0_gnn_W_msg", "L0_gnn_b_msg", "L0_gnn_W_ih", "L0_gnn_W_hh",
        "L0_gnn_b_ih", "L0_gnn_b_hh", "L1_gnn_W", "L1_gnn_b", "L2_gnn_W_src", "L2_gnn_b_src", "L2_gnn_W_dst",
        "L2_gnn_b_dst", "L2_gnn_W_v", "L2_gnn_b_v", "L3_gnn_W1", "L3_gnn_b1", "L3_gnn_W_self",
        "L3_gnn_W_neigh", "L3_gnn_b_sage", "L3_gnn_W2", "L3_gnn_b2"]


def kernel(**inputs):
    import numpy as np
    import concourse.bacc as bacc
    from concourse.bass_utils import run_bass_kernel_spmd

    nc = bacc.Bacc("TRN2", target_bir_lowering=False, num_devices=1)
    arrays, aps = {}, {}
    for name in _INS:
        arrays["in_" + name] = np.ascontiguousarray(inputs[name])
        aps[name] = nc.dram_tensor("in_" + name, arrays["in_" + name].shape,
                                   mybir.dt.from_np(arrays["in_" + name].dtype), kind="ExternalInput").ap()
    out = nc.dram_tensor("out", (N, F), mybir.dt.float32, kind="ExternalOutput").ap()
    build(nc, aps, out)
    r = run_bass_kernel_spmd(nc, [arrays], core_ids=[0])
    return r.results[0]["out"]
```

```python
import concourse.bass as bass
from concourse import mybir
from contextlib import ExitStack

N = 3125
E = 100000
P = 128
F = 128
NBR = -(-N // P)
NB = 28
NG = NB // 4
TAIL = N - (NBR - 1) * P
TILE = 128
CT = 4
CE = CT * TILE
NC = 196
R = 4
IT = NC // R
EB = 7
TR = EB * P
FULL = E // TILE
REST = E - FULL * TILE
BIG = 1e30
EPS = 1e-5
NONE = 4096


def build(nc, a, out):
    f32, bf16, i32 = mybir.dt.float32, mybir.dt.bfloat16, mybir.dt.int32
    ALU, ACT, AX = mybir.AluOpType, mybir.ActivationFunctionType, mybir.AxisListType
    ctx = ExitStack()
    with ctx:
        def sb(name, shape, dt=f32):
            return ctx.enter_context(nc.sbuf_tensor(name, shape, dt))

        def sem(name):
            return ctx.enter_context(nc.semaphore(name))

        def dram(name, shape, dt=f32):
            return nc.dram_tensor(name, shape, dt).ap()

        dst_rows = dram("dst_rows", (TR + 1, TILE), i32)
        keep_d = dram("keep_d", (TR * TILE,), bf16)
        cut_d = dram("cut_d", (TR * TILE,), bf16)
        wsum_d = dram("wsum_d", (TR * TILE, 1))
        tabs = [dram(f"tab{p}", (NB * P, F)) for p in range(4)]
        tab_sv = dram("tab_sv", (NB * P, 2 * F))
        tab_d = dram("tab_d", (NB * P, F))
        seg_d = dram("seg_d", (TR * TILE,), bf16)
        run_d = dram("run_d", (NC * CE + NB * P, F))
        frac_d = dram("frac_d", (NC * CE, 2 * F))

        X = sb("X", [P, NB, F])
        AH = sb("AH", [P, NB, 2 * F])
        A = AH[:, :, 0:F]
        H = AH[:, :, F:2 * F]
        V = sb("V", [P, NB, F])
        HTx = sb("HTx", [P, NB * P + 1])
        HT = HTx[:, 0:NB * P]
        AT = V[:, :, :].rearrange("p b c -> p (b c)")
        VT = sb("VT", [P, NB * P])
        NWB = 29
        WT = sb("WT", [P, NWB, P])
        WD = sb("WD", [P, 5, P])
        brow = sb("brow", [1, 2 * 1024 + 512])
        bcol = sb("bcol", [P, 2])
        b1bc = sb("b1bc", [P, F])
        ident = sb("ident", [P, P])
        ones = sb("ones", [P, P])
        dst_i, src_i, w_t, dst_f = (VT[:, k * TR:(k + 1) * TR].rearrange("p (b e) -> p b e", e=TILE) for k in range(4))
        dst_i, src_i = dst_i.bitcast(i32), src_i.bitcast(i32)
        src_e = sb("src_e", [P, TR])
        head_e = sb("head_e", [P, TR])
        w_e = sb("w_e", [P, TR])
        prev_i = sb("prev_i", [P, EB], i32)
        noprev = sb("noprev", [1, TILE], i32)
        prev_f = sb("prev_f", [P, EB])
        zero = sb("zero", [P, TILE], bf16)
        keep_t = sb("keep_t", [P, EB, TILE], bf16)
        cut_t = sb("cut_t", [P, EB, TILE], bf16)
        seg_t = sb("seg_t", [P, EB, TILE], bf16)
        onesb = sb("onesb", [P, TILE], bf16)
        identb = sb("identb", [P, P], bf16)
        nident = sb("nident", [P, P])
        tfirst_i = sb("tfirst_i", [P, EB], i32)
        head_i = sb("head_i", [P, NB], i32)
        nval = sb("nval", [P, NB])
        nval_i = sb("nval_i", [P, NB], i32)
        cnt = sb("cnt", [P, NB])
        cnt2 = sb("cnt2", [P, NB])
        trow = sb("trow", [P, NB])
        trow_i = sb("trow_i", [P, NB], i32)
        cum = sb("cum", [P, NB])
        last_i = sb("last_i", [P, NB], i32)
        deg = sb("deg", [P, NB])
        has = sb("has", [P, NB])
        invdeg = sb("invdeg", [P, NB])
        wlast = sb("wlast", [P, NB])
        dis = sb("dis", [P, NB])
        tmpn = sb("tmpn", [P, NB])
        mean = sb("mean", [P, NB])
        rstd = sb("rstd", [P, NB])
        tails = HTx[0:1, 0:2 * TR].rearrange("p (u t) -> p u t", u=2)
        carry = HTx[0:1, 2 * TR:3 * TR + 1]
        cprev = sb("cprev", [P, EB])
        row = HTx[0:1, :]
        degrow = sb("degrow", [1, NB * P])
        stage = sb("stage", [P, R, CT], i32)
        G = sb("G", [P, R, CT, 2 * F])
        mring = sb("mring", [P, R, CE], bf16)
        ST = sb("ST", [P, 2, CE])
        OSF = sb("OSF", [P, 2, CT, 2 * F])
        OS = OSF[:, :, :, 0:F]
        RB = sb("RB", [P, 2, CE + 1])
        D01 = sb("D01", [P, 2, 2 * CE])
        GZ = VT[:, 0:R * CE].rearrange("p (s k f) -> p s k f", s=R, f=F)
        HM = VT[:, R * CE:(R + 2) * CE].rearrange("p (s e) -> p s e", s=2)
        DN = HT[:, 0:2 * CE].rearrange("p (s e) -> p s e", s=2)
        sring = HT[:, 2 * CE:4 * CE].bitcast(bf16).rearrange("p (s e) -> p s e", s=R)
        M2 = sb("M2", [P, 2, 2, 512])
        Ee, NV = M2[:, 0, :, :], M2[:, 1, :, :]
        big = G[:, :, :, :].rearrange("p a b c -> p (a b c)")
        rgate = D01[:, 0, 0:512]
        omz = D01[:, 0, 512:1024]
        cand = D01[:, 1, 0:512]
        tnh = D01[:, 1, 512:1024]
        WN = big[:, 0:NWB * P].rearrange("p (b c) -> p b c", c=P)
        EV = big[:, 0:2 * 4 * 256].rearrange("p (s k c) -> p s k c", s=2, c=256)
        TF = M2[:, :, :, :].rearrange("p a b c -> p (a b c)")[:, 0:EB * F].rearrange("p (b f) -> p b f", f=F)
        P_t = V[:, 0:EB, :]
        lead = V[:, EB:2 * EB, :]
        fbc = V[:, 2 * EB:3 * EB, :]
        S_t = V[:, 3 * EB:4 * EB, :]
        rows_i = A.bitcast(i32)
        junk = H[:, 0:EB, :]
        head_t = H[:, EB:2 * EB, :]
        first_t = H[:, 3 * EB:4 * EB, :]
        src_f = H[:, 2 * EB:3 * EB, :]

        PS = ctx.enter_context(nc.psum_tensor("PS", [P, 8, 512], f32))

        cleared = sem("cleared")
        ld = sem("ld")
        ldw = sem("ldw")
        dpad = sem("dpad")
        prevld = sem("prevld")
        setup = sem("setup")
        cst2 = sem("cst2")
        cst = sem("cst")
        pst = sem("pst")
        maskst = sem("maskst")
        rowg = sem("rowg")
        wg = sem("wg")
        sq = sem("sq")
        h_ready = sem("h_ready")
        lnv = sem("lnv")
        lns = sem("lns")
        nstep = sem("nstep")
        tr = sem("tr")
        tre = sem("tre")
        v_ready = sem("v_ready")
        a_ready = sem("a_ready")
        agg = sem("agg")
        tabst = sem("tabst")
        attst = [sem(f"attst{q}") for q in range(2)]
        mm = sem("mm")
        mev = sem("mev")
        gr = sem("gr")
        gact = sem("gact")
        gdve = sem("gdve")
        osem = sem("osem")
        zsem = sem("zsem")
        turn = sem("turn")
        staged = sem("staged")
        gath = [sem(f"gath{h}") for h in range(R)]
        scaled = sem("scaled")
        xt = sem("xt")
        scan = sem("scan")
        back = sem("back")
        ev = sem("ev")
        odma = [sem(f"odma{q}") for q in range(2)]
        mld = [sem(f"mld{h}") for h in range(R)]
        ga = sem("ga")
        ge = sem("ge")
        gx = sem("gx")
        gfront = sem("gfront")
        gback = sem("gback")
        hm = sem("hm")
        dif = sem("dif")
        dn0 = sem("dn0")
        segm = sem("segm")
        segst = sem("segst")
        tfg = sem("tfg")
        zsc = sem("zsc")
        zt = sem("zt")
        gld = [sem(f"gld{h}") for h in range(R)]
        gstaged = sem("gstaged")
        ggath = [sem(f"ggath{h}") for h in range(R)]
        block = ctx.enter_context(nc.Block())

        SUM = [0, 1, 2, 4]

        def blocks_of(t):
            b = [("L0_gnn_W_msg", t, q, m) for q in range(2) for m in range(2)]
            b += [("L0_gnn_W_ih", t, q, m) for q in range(3) for m in range(2)]
            return b + [("L0_gnn_W_hh", t, q, 0) for q in range(3)]

        def BM(t): return t * 1024
        def BI(t): return t * 1024 + 256
        def BH(t): return t * 1024 + 640
        BQ = 2048
        B2 = 2048 + 384

        def fori(eng, p, body):
            if p == 0:
                body(0, True)
                with eng.Fori(1, IT) as i:
                    body(i, False)
            else:
                with eng.Fori(0, IT) as i:
                    body(i, False)

        @block.sync
        def _(sp):
            for t in range(2):
                o = t * 13
                sp.dma_start(WN[:, o:o + 4, :], a["L0_gnn_W_msg"][t].rearrange("(q p) (m c) -> p q m c", p=P, c=P)).then_inc(ldw, 16)
                sp.dma_start(WN[:, o + 4:o + 10, :], a["L0_gnn_W_ih"][t].rearrange("(q p) (m c) -> p q m c", p=P, c=P)).then_inc(ldw, 16)
                sp.dma_start(WN[:, o + 10:o + 13, :], a["L0_gnn_W_hh"][t].rearrange("(q p) c -> p q c", p=P)).then_inc(ldw, 16)
                sp.dma_start(brow[0:1, BM(t):BM(t) + 256], a["L0_gnn_b_msg"][t:t + 1, :]).then_inc(ldw, 16)
                sp.dma_start(brow[0:1, BI(t):BI(t) + 384], a["L0_gnn_b_ih"][t:t + 1, :]).then_inc(ldw, 16)
                sp.dma_start(brow[0:1, BH(t):BH(t) + 384], a["L0_gnn_b_hh"][t:t + 1, :]).then_inc(ldw, 16)
            for k, s in enumerate(("src", "v", "dst")):
                sp.dma_start(WN[:, 26 + k, :], a[f"L2_gnn_W_{s}"]).then_inc(ldw, 16)
                sp.dma_start(brow[0:1, BQ + k * P:BQ + k * P + P], a[f"L2_gnn_b_{s}"].rearrange("(o f) -> o f", o=1)).then_inc(ldw, 16)
            for k, s in enumerate(("L1_gnn_W", "L3_gnn_W1", "L3_gnn_W_self", "L3_gnn_W_neigh", "L3_gnn_W2")):
                sp.dma_start(WD[:, k, :], a[s]).then_inc(ldw, 16)
            sp.dma_start(brow[0:1, B2:B2 + P], a["L3_gnn_b2"].rearrange("(o f) -> o f", o=1)).then_inc(ldw, 16)
            sp.dma_start(bcol[:, 0:1], a["L3_gnn_b1"].rearrange("(f o) -> f o", o=1)).then_inc(ldw, 16)
            sp.dma_start(bcol[:, 1:2], a["L3_gnn_b_sage"].rearrange("(f o) -> f o", o=1)).then_inc(ldw, 16)
            sp.dma_start(b1bc[:, :], a["L1_gnn_b"].partition_broadcast(P)).then_inc(ldw, 16)
            sp.wait_ge(cleared, 4)
            for tile, name in ((dst_i, "dst"), (src_i, "src"), (w_t, "edge_weight")):
                nfull = FULL // P
                sp.dma_start(tile[:, 0:nfull, :], a[name][0:nfull * P * TILE].rearrange("(b p e) -> p b e", p=P, e=TILE)).then_inc(ld, 16)
                sp.dma_start(tile[0:FULL - nfull * P, nfull, :], a[name][nfull * P * TILE:FULL * TILE].rearrange("(p e) -> p e", e=TILE)).then_inc(ld, 16)
                sp.dma_start(tile[FULL - nfull * P:FULL - nfull * P + 1, nfull, 0:REST], a[name][FULL * TILE:E].rearrange("(o e) -> o e", o=1)).then_inc(ld, 16)
            sp.dma_start(X[:, 0:NBR - 1, :], a["x"][0:(NBR - 1) * P, :].rearrange("(j p) f -> p j f", p=P)).then_inc(ld, 16)
            sp.dma_start(X[0:TAIL, NBR - 1, :], a["x"][(NBR - 1) * P:N, :]).then_inc(ld, 16)
            sp.wait_ge(ld, 16 * 11)
            sp.dma_start(dst_rows[1:TR + 1, :].rearrange("(b p) e -> p b e", p=P), dst_i[:, :, :]).then_inc(dpad, 16)
            sp.dma_start(dst_rows[0:1, :], noprev[:, :]).then_inc(dpad, 16)
            sp.wait_ge(dpad, 32)
            sp.dma_start(prev_i[:, :], dst_rows[0:TR, TILE - 1:TILE].rearrange("(b p) o -> p (b o)", p=P), allow_slow_non_contiguous=True).then_inc(prevld, 16)
            sp.wait_ge(setup, 5)
            sp.dma_start(keep_d.rearrange("(b p e) -> p b e", p=P, e=TILE), keep_t[:, :, :]).then_inc(maskst, 16)
            sp.dma_start(cut_d.rearrange("(b p e) -> p b e", p=P, e=TILE), cut_t[:, :, :]).then_inc(maskst, 16)
            sp.wait_ge(segm, 1)
            sp.dma_start(seg_d.rearrange("(b p e) -> p b e", p=P, e=TILE), seg_t[:, :, :]).then_inc(segst, 16)
            sp.wait_ge(setup, 100)
            sp.dma_start(wsum_d.rearrange("(b p e) o -> p b (e o)", p=P, e=TILE), S_t).then_inc(maskst, 16)

            def prefetch(h, chunk, mask):
                sp.dma_start(mring[:, h, :], mask[bass.ds(chunk * CE, CE)].partition_broadcast(P)).then_inc(mld[h], 16)

            def edge_pass(s, mask, src_ev, src_scan):
                if s == 0:
                    sp.wait_ge(maskst, 48)
                for h in range(R):
                    if s > 0:
                        sp.wait_ge(mld[h], 16 * 50 * s)
                    prefetch(h, h, mask)

                def body(i, first):
                    for h in range(R):
                        c = i * R + h
                        src_ev(c)
                        sp.dma_start(run_d[bass.ds(c * CE, CE), :].rearrange("(k e) f -> e k f", e=TILE),
                                     OS[:, h % 2, :, :]).then_inc(odma[h % 2], 16)
                        src_scan(c)
                        prefetch(h, c + R, mask)
                fori(sp, s, body)

            def att_pass():
                sp.wait_ge(segst, 16)
                for q in range(2):
                    sp.wait_ge(mld[2 * q], 16 * 50 * 3)
                    sp.wait_ge(mld[2 * q + 1], 16 * 50 * 3)

                def load(h, c):
                    at = bass.ds(c * CE, CE)
                    sp.dma_start(GZ[:, h, :, :], run_d[at, :].rearrange("(k e) f -> e k f", e=TILE)).then_inc(gld[h], 16)
                    sp.dma_start(mring[:, h, :], cut_d[at].partition_broadcast(P)).then_inc(gld[h], 16)
                    sp.dma_start(sring[:, h, :], seg_d[at].partition_broadcast(P)).then_inc(gld[h], 16)

                def store(q, c):
                    sp.wait_ge(ev, 3 * NC + c + 1)
                    sp.dma_start(frac_d[bass.ds(c * CE, CE), :].rearrange("(k e) f -> e k f", e=TILE), OSF[:, q, :, :]).then_inc(odma[q], 16)

                for h in range(R):
                    load(h, h)

                def body(i, first, last):
                    for h in range(R):
                        c = i * R + h
                        if not last:
                            sp.wait_ge(dif, c + 1)
                            load(h, c + R)
                        if not (first and h < 1):
                            store((h + 1) % 2, c - 1)
                body(0, True, False)
                with sp.Fori(1, IT - 1) as i:
                    body(i, False, False)
                body(IT - 1, False, True)
                store((NC - 1) % 2, NC - 1)

            for r in range(2):
                sp.wait_ge(h_ready, r + 1)
                sp.dma_start(tabs[r].rearrange("(j p) f -> p j f", p=P), H[:, :, :]).then_inc(tabst, 16)
                edge_pass(r, keep_d, lambda c: sp.wait_ge(ev, r * NC + c + 1), lambda c: sp.wait_ge(scan, r * NC + c + 1))
            sp.wait_ge(mev, MEV_L1)
            sp.dma_start(tabs[2].rearrange("(j p) f -> p j f", p=P), V[:, :, :]).then_inc(tabst, 16)
            edge_pass(2, keep_d, lambda c: sp.wait_ge(ev, 2 * NC + c + 1), lambda c: sp.wait_ge(scan, 2 * NC + c + 1))
            for g in range(NG):
                sp.wait_ge(mev, MEV_L2 + g + 1)
                sp.dma_start(tab_sv[g * 512:(g + 1) * 512, :].rearrange("(k p) f -> p k f", p=P), EV[:, g % 2, :, :]).then_inc(attst[g % 2], 16)
            sp.dma_start(tab_d.rearrange("(j p) f -> p j f", p=P), V[:, :, :]).then_inc(tabst, 16)
            sp.wait_ge(zsc, 16 * NBR)
            sp.wait_ge(tfg, 16 * EB)
            at_tiles = run_d[0:NC * CE, :].rearrange("(t e) f -> t (e f)", e=TILE)[:, 0:F]
            nf = NC * CT // P
            for b in range(nf):
                sp.dma_start(at_tiles[b * P:(b + 1) * P, :], TF[:, b, :]).then_inc(zt, 16)
            sp.dma_start(at_tiles[nf * P:NC * CT, :], TF[0:NC * CT - nf * P, nf, :]).then_inc(zt, 16)
            sp.wait_ge(zt, 16 * (nf + 1))
            att_pass()
            sp.wait_ge(tre, TRE_H1N)
            sp.dma_start(tabs[3].rearrange("(j p) f -> p j f", p=P), V[:, :, :]).then_inc(tabst, 16)
            edge_pass(3, keep_d, lambda c: sp.wait_ge(ev, 4 * NC + c + 1), lambda c: sp.wait_ge(scan, 3 * NC + c + 1))
            for h in range(R):
                sp.wait_ge(mld[h], 16 * 200)
            sp.wait_ge(osem, 1)
            sp.dma_start(out[0:(NBR - 1) * P, :].rearrange("(j p) f -> p j f", p=P), X[:, 0:NBR - 1, :]).then_inc(zsem, 16)
            sp.dma_start(out[(NBR - 1) * P:N, :], X[0:TAIL, NBR - 1, :]).then_inc(zsem, 16)
            sp.wait_ge(zsem, 32)

        @block.gpsimd
        def _(pool):
            pool.memset(ident[:, :], 0.0).then_inc(cst, 1)
            pool.memset(ones[:, :], 1.0).then_inc(cst, 1)
            pool.memset(nident[:, :], 0.0).then_inc(cst2, 1)
            pool.wait_ge(cst2, 1)
            pool.affine_select(out=nident[:, :], in_=nident[:, :], compare_op=ALU.not_equal, fill=-1.0, base=0,
                               pattern=[[-1, P]], channel_multiplier=1).then_inc(cst2, 1)
            pool.iota(nval_i[:, :], pattern=[[P, NB]], base=0, channel_multiplier=1).then_inc(cst, 1)
            pool.wait_ge(cst, 1)
            pool.affine_select(out=ident[:, :], in_=ident[:, :], compare_op=ALU.not_equal, fill=1.0, base=0,
                               pattern=[[-1, P]], channel_multiplier=1).then_inc(cst, 1)

            def rows_of(dest, table, idx, done):
                pool.indirect_dma_start(dest, None, table, bass.IndirectOffsetOnAxis(ap=idx, axis=0)).then_inc(done, 16)

            pool.wait_ge(dpad, 32)
            pool.wait_ge(setup, 7)
            for j in range(NB):
                rows_of(rows_i[:, j, :], dst_rows, trow_i[:, j:j + 1], rowg)
            pool.wait_ge(setup, 102)
            pool.wait_ge(maskst, 48)
            for j in range(NB):
                rows_of(wlast[:, j:j + 1], wsum_d, last_i[:, j:j + 1], wg)

            def sum_pass(s, ntab):
                pool.wait_ge(tabst, ntab)

                def body(i, first):
                    for h in range(R):
                        pool.wait_ge(staged, s * (NC + R) + i * R + h + 1)
                        pool.sem_inc(turn, 1)
                        for k in range(CT):
                            rows_of(G[:, h, k, 0:F], tabs[s], stage[:, h, k:k + 1], gath[h])
                fori(pool, s, body)

            def att_pass():
                pool.wait_ge(mev, MEV_L2 + NG)
                for j in range(NBR):
                    pool.indirect_dma_start(run_d, bass.IndirectOffsetOnAxis(ap=head_i[:, j:j + 1], axis=0), V[:, j, :], None).then_inc(zsc, 16)
                pool.wait_ge(tabst, 64)
                for b in range(EB):
                    rows_of(TF[:, b, :], tab_d, tfirst_i[:, b:b + 1], tfg)
                for q in range(2):
                    pool.wait_ge(attst[q], 16 * ((NG + 1 - q) // 2))

                def body(i, first):
                    for h in range(R):
                        pool.wait_ge(gstaged, i * R + h + 1)
                        pool.sem_inc(turn, 1)
                        for k in range(CT):
                            rows_of(G[:, h, k, :], tab_sv, stage[:, h, k:k + 1], ggath[h])
                fori(pool, 1, body)

            def node_rows(p):
                for q in range(2):
                    pool.wait_ge(odma[q], 16 * (NC // 2) * (p + 1))
                for j in range(NBR):
                    if p == 3:
                        rows_of(AH[:, j, :], frac_d, last_i[:, j:j + 1], agg)
                    else:
                        rows_of(A[:, j, :], run_d[0:NC * CE, :], last_i[:, j:j + 1], agg)

            sum_pass(0, 16)
            node_rows(0)
            sum_pass(1, 32)
            node_rows(1)
            sum_pass(2, 48)
            node_rows(2)
            att_pass()
            node_rows(3)
            sum_pass(3, 80)
            node_rows(4)

        @block.tensor
        def _(pe):
            def turn4(bank, blocks):
                for k, b in enumerate(blocks):
                    last = nc.tensor.transpose(PS[:, bank, k * P:(k + 1) * P], b, ident[:, :])
                return last

            state = {"tr": 0}

            def turn_nodes(src, first_of=lambda g: None):
                for g in range(NG):
                    first_of(g)
                    n = state["tr"]
                    if n >= 2:
                        pe.wait_ge(tre, n - 1)
                    turn4(4 + n % 2, [src(4 * g + k) for k in range(4)]).then_inc(tr, 1)
                    state["tr"] += 1

            pe.wait_ge(cst, 4)
            pe.wait_ge(ldw, 16 * 27)
            for g in range(8):
                n = state["tr"]
                if n >= 2:
                    pe.wait_ge(tre, n - 1)
                turn4(4 + n % 2, [WN[:, b, :] for b in range(4 * g, min(4 * g + 4, NWB))]).then_inc(tr, 1)
                state["tr"] += 1
            for n, (tab, need) in enumerate(((src_f, 1), (w_t, 1))):
                pe.wait_ge(setup, need)
                pe.wait_ge(ld, 16 * 11)
                b0 = 2 * (n % 2)
                for b in range(EB):
                    last = nc.tensor.transpose(PS[:, b0 + b // 4, (b % 4) * P:(b % 4 + 1) * P], tab[:, b, :], ident[:, :])
                last.then_inc(pst, 1)
            pe.wait_ge(setup, 6)
            for b in range(EB):
                last = nc.tensor.matmul(PS[:, 6 + b // 4, (b % 4) * P:(b % 4 + 1) * P], fbc[:, b, :], ident[:, :], start=True, stop=True)
            last.then_inc(pst, 1)
            pe.wait_ge(setup, 50)
            for u, t in enumerate((P_t, lead)):
                for b in range(EB):
                    last = nc.tensor.matmul(PS[0:1, 6 + b // 4, (b % 4) * P:(b % 4 + 1) * P] if u == 0 else PS[0:1, b // 4, (b % 4) * P:(b % 4 + 1) * P],
                                            t[:, b, P - 1:P], ident[:, :], start=True, stop=True)
            last.then_inc(pst, 1)
            pe.wait_ge(setup, 51)
            for b in range(EB):
                last = nc.tensor.matmul(PS[:, 6, b:b + 1], carry[0:1, b * P:(b + 1) * P], ones[0:1, 0:1], start=True, stop=True)
            last.then_inc(pst, 1)
            pe.wait_ge(setup, 101)
            pe.wait_ge(tre, 8)
            for j in range(NB):
                last = nc.tensor.matmul(PS[0:1, j // 4, (j % 4) * P:(j % 4 + 1) * P], cum[:, j:j + 1], ident[:, :], start=True, stop=True)
            last.then_inc(pst, 1)
            pe.wait_ge(setup, 103)
            for j in range(NB):
                last = nc.tensor.matmul(PS[:, 7, j:j + 1], degrow[0:1, j * P:(j + 1) * P], ones[0:1, 0:1], start=True, stop=True)
            last.then_inc(pst, 1)
            pe.wait_ge(segm, 1)
            for b in range(EB):
                last = nc.tensor.transpose(PS[:, b // 4, (b % 4) * P:(b % 4 + 1) * P], head_t[:, b, :], ident[:, :])
            last.then_inc(pst, 1)
            pe.wait_ge(setup, 104)

            def sum_pass(s, p, weighted):
                C = s * NC
                CA = p * NC

                def body(i, first):
                    for h in range(R):
                        c, q = i * R + h, h % 2
                        if weighted:
                            pe.wait_ge(scaled, c + 1)
                        else:
                            pe.wait_ge(gath[h], 64 * (s * IT + i) + 64)
                        if not (first and h < 2):
                            pe.wait_ge(scan, C + c - 1)
                        turn4(q, [G[:, h, k, 0:F] for k in range(CT)]).then_inc(xt, 1)
                        pe.wait_ge(scan, C + c + 1)
                        if not (first and h < 2):
                            pe.wait_ge(ev, CA + c - 1)
                        turn4(2 + q, [ST[:, q, k * P:(k + 1) * P] for k in range(CT)]).then_inc(back, 1)
                fori(pe, s, body)

            def att_pass():
                pe.wait_ge(cst2, 2)

                def front(i, h, c, young):
                    q = h % 2
                    pe.wait_ge(ggath[h], 64 * i + 64)
                    pe.wait_ge(hm, c + 1)
                    if not young:
                        pe.wait_ge(gfront, GF * (c - 2) + 1)
                        pe.wait_ge(gback, GB * (c - 2) + 1)
                    for k in range(CT):
                        o = PS[:, q, k * P:(k + 1) * P]
                        nc.tensor.matmul(o, G[:, h, k, 0:F], ident[:, :], start=True, stop=False)
                        nc.tensor.matmul(o, GZ[:, h, k, :], HM[:, q, k * P:(k + 1) * P], start=False, stop=True)
                    turn4(6 + q, [G[:, h, k, F:2 * F] for k in range(CT)]).then_inc(ga, 1)

                def turn_back(q, c, young):
                    pe.wait_ge(gback, GB * c + GB)
                    pe.wait_ge(ev, 3 * NC + c)
                    turn4(2, [ST[:, q, k * P:(k + 1) * P] for k in range(CT)])
                    turn4(3, [DN[:, q, k * P:(k + 1) * P] for k in range(CT)]).then_inc(back, 1)

                def body(i, first, final):
                    for h in range(R):
                        c, q = i * R + h, h % 2
                        if not (final and h == R - 1):
                            front(i + (h + 1) // R, (h + 1) % R, c + 1, first and h < 1)
                        pe.wait_ge(gfront, GF * c + 3)
                        if not (first and h < 2):
                            pe.wait_ge(gx, c - 1)
                        nc.tensor.matmul(PS[:, 4 + q, :], ident[:, :], RB[:, q, 0:CE], start=True, stop=False)
                        nc.tensor.matmul(PS[:, 4 + q, :], nident[:, :], RB[:, q, 1:CE + 1], start=False, stop=False)
                        nc.tensor.matmul(PS[:, 4 + q, :], identb[:, :], mring[:, h, :], start=False, stop=True).then_inc(dif, 1)
                        if not (first and h < 1):
                            turn_back(1 - q, c - 1, first)
                front(0, 0, 0, True)
                body(0, True, False)
                with pe.Fori(1, IT - 1) as i:
                    body(i, False, False)
                body(IT - 1, False, True)
                turn_back((NC - 1) % 2, NC - 1, False)

            st = {"mm": 0, "gr": 0}
            for r in range(2):
                o = r * 13
                pe.wait_ge(h_ready, r + 1)
                turn_nodes(lambda b: H[:, b, :])
                pe.wait_ge(v_ready, r + 1)
                turn_nodes(lambda b: V[:, b, :])
                sum_pass(r, r, False)
                pe.wait_ge(a_ready, r + 1)
                turn_nodes(lambda b: A[:, b, :])
                pe.wait_ge(tre, state["tr"])
                for g in range(NG):
                    n = slice(g * 512, (g + 1) * 512)
                    if st["mm"]:
                        pe.wait_ge(mev, st["mm"])
                    for m in range(2):
                        nc.tensor.matmul(PS[:, 6 + m, :], WT[:, o + 2 * m, :], AT[:, n], start=True, stop=False)
                        nc.tensor.matmul(PS[:, 6 + m, :], WT[:, o + 2 * m + 1, :], VT[:, n], start=False, stop=False)
                        last = nc.tensor.matmul(PS[:, 6 + m, :], brow[0:1, BM(r) + m * P:BM(r) + (m + 1) * P], degrow[0:1, n], start=False, stop=True)
                    last.then_inc(mm, 1)
                    st["mm"] += 1
                    pe.wait_ge(mev, st["mm"])
                    if st["gr"]:
                        pe.wait_ge(gdve, 2 * st["gr"] - 1)
                    ih = WT[:, o + 4:o + 10, :].rearrange("p (q m) c -> p q m c", m=2)
                    hh = WT[:, o + 10:o + 13, :]
                    for k in range(4):
                        on = ones[0:1, :]
                        hb = HT[:, g * 512 + k * P:g * 512 + (k + 1) * P]
                        m0, m1 = (M2[:, g % 2, m, k * P:(k + 1) * P] for m in range(2))
                        rz, inn, hn = PS[:, k, 0:256], PS[:, k, 256:384], PS[:, k, 384:512]
                        nc.tensor.matmul(rz, m0, ih[:, 0:2, 0, :], start=True, stop=False)
                        nc.tensor.matmul(rz, m1, ih[:, 0:2, 1, :], start=False, stop=False)
                        nc.tensor.matmul(rz, hb, hh[:, 0:2, :], start=False, stop=False)
                        nc.tensor.matmul(rz, on, brow[0:1, BI(r):BI(r) + 256], start=False, stop=False)
                        nc.tensor.matmul(rz, on, brow[0:1, BH(r):BH(r) + 256], start=False, stop=True)
                        nc.tensor.matmul(inn, m0, ih[:, 2, 0, :], start=True, stop=False)
                        nc.tensor.matmul(inn, m1, ih[:, 2, 1, :], start=False, stop=False)
                        nc.tensor.matmul(inn, on, brow[0:1, BI(r) + 256:BI(r) + 384], start=False, stop=True)
                        nc.tensor.matmul(hn, hb, hh[:, 2, :], start=True, stop=False)
                        last = nc.tensor.matmul(hn, on, brow[0:1, BH(r) + 256:BH(r) + 384], start=False, stop=True)
                    last.then_inc(gr, 1)
                    st["gr"] += 1
            pe.wait_ge(h_ready, 3)
            turn_nodes(lambda b: H[:, b, :])
            pe.wait_ge(tre, state["tr"])

            def product(groups, banks, lag):
                for g in range(NG):
                    if st["mm"]:
                        pe.wait_ge(mev, st["mm"] - lag)
                    groups(g).then_inc(mm, 1)
                    st["mm"] += 1

            def xw(g):
                for k in range(4):
                    last = nc.tensor.matmul(PS[:, 6 + g % 2, k * P:(k + 1) * P], HT[:, g * 512 + k * P:g * 512 + (k + 1) * P], WD[:, 0, :], start=True, stop=True)
                return last
            product(xw, None, 0)
            sum_pass(2, 2, True)
            pe.wait_ge(h_ready, 4)
            turn_nodes(lambda b: H[:, b, :])
            pe.wait_ge(tre, state["tr"])

            def qkv(g):
                for k in range(4):
                    nc.tensor.matmul(PS[:, k, 0:384], HT[:, g * 512 + k * P:g * 512 + (k + 1) * P], WT[:, 26:29, :], start=True, stop=False)
                    last = nc.tensor.matmul(PS[:, k, 0:384], ones[0:1, :], brow[0:1, BQ:BQ + 384], start=False, stop=True)
                return last
            product(qkv, None, 0)
            pe.wait_ge(mev, st["mm"])
            att_pass()
            pe.wait_ge(h_ready, 5)
            turn_nodes(lambda b: H[:, b, :])
            pe.wait_ge(tre, state["tr"])
            product(lambda g: nc.tensor.matmul(PS[:, 6 + g % 2, :], WD[:, 1, :], HT[:, g * 512:(g + 1) * 512], start=True, stop=True), None, 0)
            pe.wait_ge(mev, st["mm"])
            turn_nodes(lambda b: VT[:, b * P:(b + 1) * P])
            assert state["tr"] == TRE_H1N
            sum_pass(3, 4, False)
            pe.wait_ge(a_ready, 3)
            turn_nodes(lambda b: A[:, b, :])
            pe.wait_ge(tre, state["tr"])

            def hidden(g):
                nc.tensor.matmul(PS[:, 6 + g % 2, :], WD[:, 2, :], VT[:, g * 512:(g + 1) * 512], start=True, stop=False)
                return nc.tensor.matmul(PS[:, 6 + g % 2, :], WD[:, 3, :], AT[:, g * 512:(g + 1) * 512], start=False, stop=True)
            product(hidden, None, 0)
            pe.wait_ge(mev, st["mm"])

            def last_product(g):
                for k in range(4):
                    nc.tensor.matmul(PS[:, 6 + g % 2, k * P:(k + 1) * P], HT[:, g * 512 + k * P:g * 512 + (k + 1) * P], WD[:, 4, :], start=True, stop=False)
                    last = nc.tensor.matmul(PS[:, 6 + g % 2, k * P:(k + 1) * P], ones[0:1, :], brow[0:1, B2:B2 + P], start=False, stop=True)
                return last
            product(last_product, None, 0)

        @block.scalar
        def _(act):
            state = {"tr": 0, "mm": 0, "gr": 0}

            def take(dests):
                for d in dests:
                    n = state["tr"]
                    act.wait_ge(tr, n + 1)
                    nc.scalar.activation(d, PS[:, 4 + n % 2, 0:d.free_size()], ACT.Copy).then_inc(tre, 1)
                    state["tr"] += 1

            def groups(t):
                return [t[:, g * 512:(g + 1) * 512] for g in range(NG)]

            wt = WT[:, :, :].rearrange("p b c -> p (b c)")
            take([wt[:, g * 512:min((g + 1) * 512, NWB * P)] for g in range(8)])
            act.wait_ge(setup, 105)
            nc.scalar.activation(dis[:, :], tmpn[:, :], ACT.Sqrt).then_inc(sq, 1)

            def ln_sqrt(n):
                act.wait_ge(lnv, n)
                nc.scalar.activation(rstd[:, 0:NBR], tmpn[:, 0:NBR], ACT.Sqrt).then_inc(lns, 1)

            def sum_pass(s, p, weighted):
                CA = p * NC

                def body(i, first):
                    for h in range(R):
                        c, q = i * R + h, h % 2
                        if weighted:
                            act.wait_ge(gath[h], 64 * (s * IT + i) + 64)
                            act.sem_inc(turn, 1)
                            for k in range(CT):
                                last = nc.scalar.activation(G[:, h, k, 0:F], G[:, h, k, 0:F], ACT.Copy, scale=w_e[:, bass.ds(c * CT + k, 1)])
                            last.then_inc(scaled, 1)
                        act.wait_ge(back, CA + c + 1)
                        if not (first and h < 2):
                            act.wait_ge(odma[q], 16 * (p * (NC // 2) + i * 2 + h // 2))
                        nc.scalar.activation(OS[:, q, :, :], PS[:, 2 + q, :].rearrange("p (k f) -> p k f", f=F), ACT.Copy).then_inc(ev, 1)
                fori(act, s, body)

            def att_pass():
                def fifth(q, c, young):
                    act.wait_ge(ga, c + 1)
                    if not young:
                        act.wait_ge(gfront, GF * (c - 2) + GF)
                    nc.scalar.activation(Ee[:, q, :], PS[:, q, :], ACT.Copy, scale=0.2).then_inc(ge, 1)

                def take_out(q, c, k):
                    act.wait_ge(back, 3 * NC + c + 1)
                    act.wait_ge(odma[q], 16 * k)
                    for b, o in ((2, 0), (3, F)):
                        last = nc.scalar.activation(OSF[:, q, :, o:o + F], PS[:, b, :].rearrange("p (k f) -> p k f", f=F), ACT.Copy)
                    last.then_inc(ev, 1)

                def body(i, first, final):
                    for h in range(R):
                        c, q = i * R + h, h % 2
                        if not (final and h == R - 1):
                            fifth(1 - q, c + 1, first and h < 1)
                        act.wait_ge(dif, c + 1)
                        if not (first and h < 2):
                            act.wait_ge(gback, GB * (c - 2) + GB)
                        nc.scalar.activation(D01[:, q, 0:CE], PS[:, 4 + q, :], ACT.Exp)
                        act.wait_ge(gfront, GF * c + GF)
                        nc.scalar.activation(D01[:, q, CE:2 * CE], D01[:, q, CE:2 * CE], ACT.Exp).then_inc(gx, 1)
                        if not (first and h < 1):
                            take_out(1 - q, c - 1, 3 * (NC // 2) + i * 2 + (h + 1) // 2 - 1)
                fifth(0, 0, True)
                body(0, True, False)
                with act.Fori(1, IT - 1) as i:
                    body(i, False, False)
                body(IT - 1, False, True)
                take_out((NC - 1) % 2, NC - 1, 4 * (NC // 2) - 1)

            ln_sqrt(1)
            for r in range(2):
                take(groups(HT))
                take(groups(VT))
                sum_pass(r, r, False)
                take(groups(AT))
                for g in range(NG):
                    act.wait_ge(mm, state["mm"] + 1)
                    if state["gr"] >= 2:
                        act.wait_ge(gr, state["gr"] - 1)
                    nc.scalar.activation(M2[:, g % 2, :, :], PS[:, 6:8, :], ACT.Copy).then_inc(mev, 1)
                    state["mm"] += 1
                    state["gr"] += 1
                    act.wait_ge(gr, state["gr"])
                    if state["gr"] > 1:
                        act.wait_ge(gdve, 2 * (state["gr"] - 1))
                    nc.scalar.activation(rgate.rearrange("p (k c) -> p k c", c=P), PS[:, 0:4, 0:128], ACT.Sigmoid)
                    nc.scalar.activation(omz.rearrange("p (k c) -> p k c", c=P), PS[:, 0:4, 128:256], ACT.Sigmoid, scale=-1.0).then_inc(gact, 1)
                    act.wait_ge(gdve, 2 * state["gr"] - 1)
                    nc.scalar.activation(tnh, cand, ACT.Tanh).then_inc(gact, 1)
            ln_sqrt(2)
            take(groups(HT))
            for g in range(NG):
                act.wait_ge(mm, state["mm"] + 1)
                for k in range(4):
                    last = nc.scalar.activation(V[:, 4 * g + k, :], PS[:, 6 + g % 2, k * P:(k + 1) * P], ACT.Copy, scale=dis[:, 4 * g + k:4 * g + k + 1])
                last.then_inc(mev, 1)
                state["mm"] += 1
            assert state["mm"] == MEV_L1
            sum_pass(2, 2, True)
            ln_sqrt(3)
            take(groups(HT))
            for g in range(NG):
                act.wait_ge(mm, state["mm"] + 1)
                if g >= 2:
                    act.wait_ge(attst[g % 2], 16 * (g // 2))
                nc.scalar.activation(EV[:, g % 2, :, :], PS[:, 0:4, 0:256], ACT.Copy)
                nc.scalar.activation(V[:, 4 * g:4 * g + 4, :], PS[:, 0:4, 256:384], ACT.Copy).then_inc(mev, 1)
                state["mm"] += 1
            att_pass()
            ln_sqrt(4)
            take(groups(HT))
            for g in range(NG):
                act.wait_ge(mm, state["mm"] + 1)
                nc.scalar.activation(VT[:, g * 512:(g + 1) * 512], PS[:, 6 + g % 2, :], ACT.Relu, bias=bcol[:, 0:1]).then_inc(mev, 1)
                state["mm"] += 1
            take([V[:, 4 * g:4 * g + 4, :] for g in range(NG)])
            sum_pass(3, 4, False)
            take(groups(AT))
            for g in range(NG):
                act.wait_ge(mm, state["mm"] + 1)
                nc.scalar.activation(HT[:, g * 512:(g + 1) * 512], PS[:, 6 + g % 2, :], ACT.Relu, bias=bcol[:, 1:2]).then_inc(mev, 1)
                state["mm"] += 1
            for g in range(NG):
                act.wait_ge(mm, state["mm"] + 1)
                nc.scalar.activation(H[:, 4 * g:4 * g + 4, :], PS[:, 6 + g % 2, :].rearrange("p (k c) -> p k c", c=P), ACT.Relu).then_inc(mev, 1)
                state["mm"] += 1

        @block.vector
        def _(dve):
            chain = {"n": 0}

            def step(ins):
                chain["n"] += 1
                ins.then_inc(nstep, 1)
                dve.wait_ge(nstep, chain["n"])

            v = nc.vector
            v.memset(dst_i[:, :, :], NONE)
            v.memset(src_i[:, :, :], 0)
            v.memset(noprev[:, :], -1)
            v.memset(w_t[:, :, :], 0.0).then_inc(cleared, 2)
            step(v.memset(onesb[:, :], 1.0))
            v.memset(X[:, NBR - 1:NB, :], 0.0).then_inc(cleared, 2)
            step(v.memset(carry[:, 0:1], 0.0))
            step(v.memset(zero[:, :], 0.0))
            step(v.memset(ST[:, :, :], 0.0))
            step(v.memset(RB[:, :, :], 0.0))
            dve.wait_ge(cleared, 4)
            dve.wait_ge(ld, 16 * 11)
            v.tensor_copy(src_f, src_i[:, :, :]).then_inc(setup, 1)
            step(v.tensor_copy(dst_f[:, :, :], dst_i[:, :, :]))
            step(v.tensor_scalar(prev_f[:, :], dst_f[:, :, 0], float(NB * P - 1), None, ALU.min))
            step(v.tensor_copy(tfirst_i[:, :], prev_f[:, :]))
            dve.wait_ge(cst, 4)
            dve.wait_ge(pst, 1)
            pv = PS[:, :, :].rearrange("p b c -> p (b c)")
            v.tensor_copy(src_e[:, :], pv[:, 0:TR]).then_inc(setup, 3)
            step(v.tensor_copy(identb[:, :], ident[:, :]))
            dve.wait_ge(prevld, 16)
            step(v.tensor_copy(prev_f[:, :], prev_i[:, :]))
            v.tensor_tensor(keep_t[:, :, 1:TILE], dst_f[:, :, 1:TILE], dst_f[:, :, 0:TILE - 1], ALU.is_equal)
            step(v.tensor_tensor(keep_t[:, :, 0], dst_f[:, :, 0], prev_f[:, :], ALU.is_equal))
            v.tensor_scalar(cut_t[:, :, :], keep_t[:, :, :], BIG, -BIG, ALU.mult, ALU.add).then_inc(setup, 1)
            v.tensor_copy(fbc, dst_f[:, :, 0:1].to_broadcast([P, EB, P])).then_inc(setup, 1)
            step(v.tensor_copy(nval[:, :], nval_i[:, :]))
            step(v.tensor_scalar(src_f, keep_t[:, :, :], -1.0, 1.0, ALU.mult, ALU.add))
            step(v.memset(src_f[:, :, 0], 0.0))
            for b in range(EB):
                step(v.tensor_tensor_scan(first_t[:, b, :], onesb[:, :], src_f[:, b, :], 0.0, ALU.mult, ALU.add))
            step(v.tensor_copy(seg_t[:, :, :], first_t))
            step(v.memset(src_f[:, :, 0], 1.0))
            step(v.scalar_tensor_tensor(head_t, first_t, 1.0, src_f, ALU.add, ALU.mult))
            v.tensor_scalar(head_t, head_t, -1.0, None, ALU.add).then_inc(segm, 1)
            dve.wait_ge(pst, 2)
            step(v.tensor_copy(w_e[:, :], pv[:, 1024:1024 + TR]))
            dve.wait_ge(pst, 3)
            for j in range(NB):
                step(v.tensor_scalar(junk, pv[:, 3072:3072 + TR].rearrange("p (b e) -> p b e", e=TILE), nval[:, j:j + 1], 0.0, ALU.is_le, ALU.add, accum_out=cnt[:, j:j + 1]))
            step(v.tensor_scalar(trow[:, :], cnt[:, :], 1.0, 1.0, ALU.max, ALU.mult))
            v.tensor_copy(trow_i[:, :], trow[:, :]).then_inc(setup, 1)
            for b in range(EB):
                v.tensor_tensor_scan(P_t[:, b, :], keep_t[:, b, :], w_t[:, b, :], 0.0, ALU.mult, ALU.add)
                last = v.tensor_tensor_scan(lead[:, b, :], keep_t[:, b, :], zero[:, :], 1.0, ALU.mult, ALU.add)
            last.then_inc(setup, 43)
            dve.wait_ge(pst, 4)
            v.tensor_copy(tails[:, 0, :], pv[0:1, 3072:3072 + TR])
            step(v.tensor_copy(tails[:, 1, :], pv[0:1, 0:TR]))
            v.tensor_tensor_scan(carry[:, 1:TR + 1], tails[:, 1, :], tails[:, 0, :], 0.0, ALU.mult, ALU.add).then_inc(setup, 1)
            dve.wait_ge(pst, 5)
            step(v.tensor_copy(cprev[:, :], PS[:, 6, 0:EB]))
            for b in range(EB):
                last = v.scalar_tensor_tensor(S_t[:, b, :], lead[:, b, :], cprev[:, b:b + 1], P_t[:, b, :], ALU.mult, ALU.add)
            last.then_inc(setup, 49)
            dve.wait_ge(rowg, 16 * NB)
            for j in range(NB):
                step(v.tensor_scalar(junk[:, 0, :], rows_i[:, j, :], nval[:, j:j + 1], 0.0, ALU.is_le, ALU.add, accum_out=cnt2[:, j:j + 1]))
            step(v.tensor_scalar(trow[:, :], trow[:, :], -1.0, float(TILE), ALU.add, ALU.mult))
            v.tensor_tensor(cum[:, :], trow[:, :], cnt2[:, :], ALU.add).then_inc(setup, 1)
            dve.wait_ge(setup, 101)
            step(v.tensor_scalar(trow[:, :], cum[:, :], -1.0, 0.0, ALU.add, ALU.max))
            v.tensor_copy(last_i[:, :], trow[:, :]).then_inc(setup, 1)
            dve.wait_ge(pst, 6)
            step(v.memset(row[:, 0:1], 0.0))
            step(v.tensor_copy(row[:, 1:NB * P + 1], pv[0:1, 0:NB * P]))
            v.tensor_tensor(degrow[:, :], row[:, 1:NB * P + 1], row[:, 0:NB * P], ALU.subtract).then_inc(setup, 1)
            dve.wait_ge(pst, 7)
            v.tensor_copy(deg[:, :], PS[:, 7, 0:NB]).then_inc(setup, 1)
            dve.wait_ge(setup, 104)
            step(v.tensor_scalar(has[:, :], deg[:, :], 1.0, None, ALU.min))
            step(v.tensor_tensor(cum[:, :], cum[:, :], deg[:, :], ALU.subtract))
            step(v.tensor_scalar(trow[:, :], nval[:, :], float(NC * CE), None, ALU.add))
            step(v.tensor_tensor(cum[:, :], cum[:, :], trow[:, :], ALU.subtract))
            step(v.tensor_tensor(cum[:, :], cum[:, :], has[:, :], ALU.mult))
            step(v.tensor_tensor(cum[:, :], cum[:, :], trow[:, :], ALU.add))
            step(v.tensor_copy(head_i[:, :], cum[:, :]))
            dve.wait_ge(pst, 8)
            step(v.tensor_copy(head_e[:, :], pv[:, 0:TR]))
            step(v.memset(H[:, NBR:NB, :], 0.0))
            step(v.tensor_scalar(invdeg[:, :], deg[:, :], 1.0, None, ALU.max))
            step(v.reciprocal(invdeg[:, :], invdeg[:, :]))
            step(v.tensor_tensor(invdeg[:, :], invdeg[:, :], has[:, :], ALU.mult))
            dve.wait_ge(wg, 16 * NB)
            step(v.tensor_tensor(wlast[:, :], wlast[:, :], has[:, :], ALU.mult))
            step(v.tensor_scalar(wlast[:, :], wlast[:, :], 1.0, None, ALU.add))
            step(v.tensor_scalar(tmpn[:, :], wlast[:, :], 1e-30, None, ALU.max))
            v.reciprocal(tmpn[:, :], tmpn[:, :]).then_inc(setup, 1)
            step(v.tensor_scalar(wlast[:, :], wlast[:, :], 0.0, None, ALU.is_gt))
            dve.wait_ge(sq, 1)
            step(v.tensor_tensor(dis[:, :], dis[:, :], wlast[:, :], ALU.mult))

            def bc(t):
                return t[:, 0:NBR].unsqueeze(2).to_broadcast([P, NBR, F])

            def bcn(t):
                return t[:, :].unsqueeze(2).to_broadcast([P, NB, F])

            def layernorm(n):
                x, c, h = X[:, 0:NBR, :], A[:, 0:NBR, :], H[:, 0:NBR, :]
                step(v.tensor_reduce(mean[:, 0:NBR], x, AX.X, ALU.add))
                step(v.tensor_scalar(mean[:, 0:NBR], mean[:, 0:NBR], 1.0 / F, None, ALU.mult))
                step(v.tensor_tensor(c, x, bc(mean), ALU.subtract))
                step(v.tensor_tensor(h, c, c, ALU.mult))
                step(v.tensor_reduce(tmpn[:, 0:NBR], h, AX.X, ALU.add))
                v.tensor_scalar(tmpn[:, 0:NBR], tmpn[:, 0:NBR], 1.0 / F, EPS, ALU.mult, ALU.add).then_inc(lnv, 1)
                dve.wait_ge(lns, n)
                step(v.reciprocal(rstd[:, 0:NBR], rstd[:, 0:NBR]))
                v.scalar_tensor_tensor(h, c, 0.0, bc(rstd), ALU.max, ALU.mult).then_inc(h_ready, 1)

            def stage_ahead(h, tile, done):
                v.tensor_scalar(stage[:, h, :], src_e[:, bass.ds(tile, CT)], 0.0, None, ALU.add).then_inc(done, 1)

            def sum_pass(s, p):
                C = s * NC
                if s:
                    dve.wait_ge(staged, s * (NC + R))
                for h in range(R):
                    stage_ahead(h, h * CT, staged)

                def body(i, first):
                    for h in range(R):
                        c, q = i * R + h, h % 2
                        dve.wait_ge(mld[h], 16 * (50 * s + i) + 16)
                        dve.wait_ge(xt, C + c + 1)
                        if not (first and h < 2):
                            dve.wait_ge(back, p * NC + c - 1)
                        if not (first and h < 1):
                            dve.wait_ge(scan, C + c)
                        v.tensor_tensor_scan(ST[:, q, :], mring[:, h, :], PS[:, q, :], ST[:, 1 - q, CE - 1:CE], ALU.mult, ALU.add).then_inc(scan, 1)
                        stage_ahead(h, (c + R) * CT, staged)
                fori(dve, s, body)

            def att_pass():
                dve.wait_ge(staged, 3 * (NC + R))
                dve.wait_ge(tre, TRE_L2)
                dve.wait_ge(mm, MEV_L2 + NG)
                for h in range(R):
                    stage_ahead(h, h * CT, gstaged)
                v.memset(DN, 0.0).then_inc(dn0, 1)
                dve.wait_ge(dn0, 1)

                def heads(i, h, c):
                    dve.wait_ge(gld[h], 48 * i + 48)
                    v.tensor_tensor(HM[:, h % 2, :].rearrange("p (k e) -> p k e", e=TILE),
                                    sring[:, h, :].rearrange("p (k e) -> p k e", e=TILE),
                                    head_e[:, bass.ds(c * CT, CT)].unsqueeze(2).to_broadcast([P, CT, TILE]),
                                    ALU.is_equal).then_inc(hm, 1)

                def part_a(i, h, c, young, chunk0, final):
                    q = h % 2
                    dve.wait_ge(ge, c + 1)
                    v.tensor_tensor(Ee[:, q, :], PS[:, q, :], Ee[:, q, :], ALU.max).then_inc(gfront, 1)
                    v.tensor_copy(RB[:, q, 0:1], RB[:, 1 - q, CE:CE + 1]).then_inc(gfront, 1)
                    dve.wait_ge(gfront, GF * c + 2)
                    v.tensor_tensor_scan(RB[:, q, 1:CE + 1], mring[:, h, :], Ee[:, q, :], RB[:, q, 0:1], ALU.add, ALU.max).then_inc(gfront, 1)
                    if not (final and h >= 2):
                        heads(i + (h + 2) // R, (h + 2) % R, c + 2)
                    stage_ahead(h, (c + R) * CT, gstaged)
                    dve.wait_ge(gfront, GF * c + 3)
                    if not young:
                        dve.wait_ge(gback, GB * (c - 2) + GB)
                    v.tensor_tensor(D01[:, q, CE:2 * CE], Ee[:, q, :], RB[:, q, 1:CE + 1], ALU.subtract).then_inc(gfront, 1)

                def part_b(q, c, young, chunk0):
                    dve.wait_ge(gx, c + 1)
                    v.tensor_tensor(NV[:, q, :], D01[:, q, CE:2 * CE], PS[:, 6 + q, :], ALU.mult).then_inc(gback, 1)
                    if not young:
                        dve.wait_ge(back, 3 * NC + c - 1)
                    if not chunk0:
                        dve.wait_ge(gback, GB * c)
                    v.tensor_tensor_scan(DN[:, q, :], D01[:, q, 0:CE], D01[:, q, CE:2 * CE], DN[:, 1 - q, CE - 1:CE], ALU.mult, ALU.add).then_inc(gback, 1)
                    dve.wait_ge(gback, GB * c + 1)
                    v.tensor_tensor_scan(ST[:, q, :], D01[:, q, 0:CE], NV[:, q, :], ST[:, 1 - q, CE - 1:CE], ALU.mult, ALU.add).then_inc(gback, 1)

                def body(i, first, final):
                    for h in range(R):
                        c = i * R + h
                        part_a(i, h, c, first and h < 2, first and h < 1, final)
                        if not (first and h < 1):
                            part_b(1 - h % 2, c - 1, first and h < 3, first and h < 2)
                heads(0, 0, 0)
                heads(0, 1, 1)
                body(0, True, False)
                with dve.Fori(1, IT - 1) as i:
                    body(i, False, False)
                body(IT - 1, False, True)
                part_b((NC - 1) % 2, NC - 1, False, False)

            layernorm(1)
            st = {"gr": 0}
            for r in range(2):
                dve.wait_ge(h_ready, r + 1)
                if r == 0:
                    dve.wait_ge(maskst, 48)
                    dve.wait_ge(wg, 16 * NB)
                else:
                    dve.wait_ge(tre, 8 + 3 * NG)
                v.tensor_tensor(V[:, :, :], H[:, :, :], bcn(deg), ALU.mult).then_inc(v_ready, 1)
                if r == 0:
                    step(v.memset(A[:, NBR:NB, :], 0.0))
                sum_pass(r, r)
                dve.wait_ge(agg, 16 * NBR * (r + 1))
                v.tensor_tensor(A[:, 0:NBR, :], A[:, 0:NBR, :], bc(has), ALU.mult).then_inc(a_ready, 1)
                dve.wait_ge(tabst, 16 * (r + 1))
                for g in range(NG):
                    n = st["gr"]
                    kk = slice(4 * g, 4 * g + 4)
                    dve.wait_ge(gact, 2 * n + 1)
                    cd = cand.rearrange("p (k c) -> p k c", c=P)
                    tn = tnh.rearrange("p (k c) -> p k c", c=P)
                    oz = omz.rearrange("p (k c) -> p k c", c=P)
                    step(v.tensor_tensor(cd, rgate.rearrange("p (k c) -> p k c", c=P), PS[:, 0:4, 384:512], ALU.mult))
                    v.tensor_tensor(cd, cd, PS[:, 0:4, 256:384], ALU.add).then_inc(gdve, 1)
                    dve.wait_ge(gact, 2 * n + 2)
                    step(v.tensor_tensor(tn, tn, H[:, kk, :], ALU.subtract))
                    step(v.tensor_tensor(tn, tn, oz, ALU.mult))
                    step(v.tensor_tensor(tn, tn, has[:, kk].unsqueeze(2).to_broadcast([P, 4, F]), ALU.mult))
                    v.tensor_tensor(H[:, kk, :], H[:, kk, :], tn, ALU.add).then_inc(gdve, 1)
                    st["gr"] += 1
                dve.wait_ge(gdve, 2 * st["gr"])
                if r == 0:
                    dve.sem_inc(h_ready, 1)
            step(v.tensor_tensor(X[:, 0:NBR, :], X[:, 0:NBR, :], H[:, 0:NBR, :], ALU.add))
            layernorm(2)
            dve.wait_ge(h_ready, 3)

            sum_pass(2, 2)
            dve.wait_ge(agg, 16 * NBR * 3)
            dve.wait_ge(tabst, 48)
            r_ = slice(0, NBR)
            step(v.tensor_tensor(A[:, r_, :], A[:, r_, :], bc(has), ALU.mult))
            step(v.tensor_tensor(A[:, r_, :], A[:, r_, :], V[:, r_, :], ALU.add))
            step(v.tensor_tensor(A[:, r_, :], A[:, r_, :], bc(dis), ALU.mult))
            step(v.tensor_tensor(A[:, r_, :], A[:, r_, :], b1bc[:, :].unsqueeze(1).to_broadcast([P, NBR, F]), ALU.add))
            step(v.tensor_tensor(X[:, r_, :], X[:, r_, :], A[:, r_, :], ALU.add))
            layernorm(3)
            dve.wait_ge(h_ready, 4)

            att_pass()
            dve.wait_ge(agg, 16 * NBR * 4)
            step(v.reciprocal(H[:, r_, :], H[:, r_, :]))
            step(v.tensor_tensor(A[:, r_, :], A[:, r_, :], H[:, r_, :], ALU.mult))
            step(v.tensor_tensor(A[:, r_, :], A[:, r_, :], bc(has), ALU.mult))
            step(v.tensor_tensor(X[:, r_, :], X[:, r_, :], A[:, r_, :], ALU.add))
            layernorm(4)
            dve.wait_ge(h_ready, 5)

            sum_pass(3, 4)
            dve.wait_ge(agg, 16 * NBR * 5)
            v.tensor_tensor(A[:, r_, :], A[:, r_, :], bc(invdeg), ALU.mult).then_inc(a_ready, 1)
            dve.wait_ge(mev, MEV_L1 + 4 * NG)
            v.tensor_tensor(X[:, r_, :], X[:, r_, :], H[:, r_, :], ALU.add).then_inc(osem, 1)


MEV_L1 = 3 * NG
MEV_L2 = 3 * NG
TRE_H1N = 8 + 10 * NG
TRE_L2 = 8 + 8 * NG
GF, GB = 4, 3


_INS = ["x", "src", "dst", "edge_weight", "L0_gnn_W_msg", "L0_gnn_b_msg", "L0_gnn_W_ih", "L0_gnn_W_hh",
        "L0_gnn_b_ih", "L0_gnn_b_hh", "L1_gnn_W", "L1_gnn_b", "L2_gnn_W_src", "L2_gnn_b_src", "L2_gnn_W_dst",
        "L2_gnn_b_dst", "L2_gnn_W_v", "L2_gnn_b_v", "L3_gnn_W1", "L3_gnn_b1", "L3_gnn_W_self",
        "L3_gnn_W_neigh", "L3_gnn_b_sage", "L3_gnn_W2", "L3_gnn_b2"]


def kernel(**inputs):
    import numpy as np
    import concourse.bacc as bacc
    from concourse.bass_utils import run_bass_kernel_spmd

    nc = bacc.Bacc("TRN2", target_bir_lowering=False, num_devices=1)
    arrays, aps = {}, {}
    for name in _INS:
        arrays["in_" + name] = np.ascontiguousarray(inputs[name])
        aps[name] = nc.dram_tensor("in_" + name, arrays["in_" + name].shape,
                                   mybir.dt.from_np(arrays["in_" + name].dtype), kind="ExternalInput").ap()
    out = nc.dram_tensor("out", (N, F), mybir.dt.float32, kind="ExternalOutput").ap()
    build(nc, aps, out)
    r = run_bass_kernel_spmd(nc, [arrays], core_ids=[0])
    return r.results[0]["out"]
```

```python
import concourse.bass as bass
from concourse import mybir
from contextlib import ExitStack

N = 3125
E = 100000
P = 128
F = 128
NBR = -(-N // P)
NB = 28
NG = NB // 4
TAIL = N - (NBR - 1) * P
TILE = 128
CT = 4
CE = CT * TILE
NC = 196
R = 4
IT = NC // R
EB = 7
TR = EB * P
FULL = E // TILE
REST = E - FULL * TILE
BIG = 1e30
EPS = 1e-5
NONE = 4096


def build(nc, a, out):
    f32, bf16, i32 = mybir.dt.float32, mybir.dt.bfloat16, mybir.dt.int32
    ALU, ACT, AX = mybir.AluOpType, mybir.ActivationFunctionType, mybir.AxisListType
    ctx = ExitStack()
    with ctx:
        def sb(name, shape, dt=f32):
            return ctx.enter_context(nc.sbuf_tensor(name, shape, dt))

        def sem(name):
            return ctx.enter_context(nc.semaphore(name))

        def dram(name, shape, dt=f32):
            return nc.dram_tensor(name, shape, dt).ap()

        dst_rows = dram("dst_rows", (TR + 1, TILE), i32)
        keep_d = dram("keep_d", (TR * TILE,), bf16)
        cut_d = dram("cut_d", (TR * TILE,), bf16)
        wsum_d = dram("wsum_d", (TR * TILE, 1))
        tabs = [dram(f"tab{p}", (NBR * P, F)) for p in range(4)]
        tab_sv = dram("tab_sv", (NBR * P, 2 * F))
        tab_d = dram("tab_d", (NBR * P, F))
        seg_d = dram("seg_d", (TR * TILE,), bf16)
        run_d = dram("run_d", (NC * CE + NB * P, F))
        frac_d = dram("frac_d", (NC * CE, 2 * F))

        X = sb("X", [P, NB, F])
        AH = sb("AH", [P, NB, 2 * F])
        A = AH[:, :, 0:F]
        H = AH[:, :, F:2 * F]
        V = sb("V", [P, NB, F])
        HTx = sb("HTx", [P, NB * P + 1])
        HT = HTx[:, 0:NB * P]
        AT = V[:, :, :].rearrange("p b c -> p (b c)")
        VT = sb("VT", [P, NB * P])
        NWB = 29
        WT = sb("WT", [P, NWB, P])
        WD = sb("WD", [P, 5, P])
        brow = sb("brow", [1, 512])
        bmcol = sb("bmcol", [P, 2, 2])
        US = sb("US", [P, 2, 2, 3 * P])
        bgate = sb("bgate", [3, 2, 512])
        bcol = sb("bcol", [P, 2])
        b1bc = sb("b1bc", [P, F])
        ident = sb("ident", [P, P])
        ones = sb("ones", [P, P])
        dst_i, src_i, w_t, dst_f = (VT[:, k * TR:(k + 1) * TR].rearrange("p (b e) -> p b e", e=TILE) for k in range(4))
        dst_i, src_i = dst_i.bitcast(i32), src_i.bitcast(i32)
        src_e = sb("src_e", [P, TR])
        head_e = sb("head_e", [P, TR])
        w_e = sb("w_e", [P, TR])
        prev_i = sb("prev_i", [P, EB], i32)
        noprev = sb("noprev", [1, TILE], i32)
        prev_f = sb("prev_f", [P, EB])
        zero = sb("zero", [P, TILE], bf16)
        keep_t = sb("keep_t", [P, EB, TILE], bf16)
        cut_t = sb("cut_t", [P, EB, TILE], bf16)
        seg_t = sb("seg_t", [P, EB, TILE], bf16)
        onesb = sb("onesb", [P, TILE], bf16)
        identb = sb("identb", [P, P], bf16)
        nident = sb("nident", [P, P])
        tfirst_i = sb("tfirst_i", [P, EB], i32)
        head_i = sb("head_i", [P, NB], i32)
        nval = sb("nval", [P, NB])
        nval_i = sb("nval_i", [P, NB], i32)
        cnt = sb("cnt", [P, NB])
        cnt2 = sb("cnt2", [P, NB])
        trow = sb("trow", [P, NB])
        trow_i = sb("trow_i", [P, NB], i32)
        cum = sb("cum", [P, NB])
        last_i = sb("last_i", [P, NB], i32)
        deg = sb("deg", [P, NB])
        has = sb("has", [P, NB])
        invdeg = sb("invdeg", [P, NB])
        wlast = sb("wlast", [P, NB])
        dis = sb("dis", [P, NB])
        tmpn = sb("tmpn", [P, NB])
        mean = sb("mean", [P, NB])
        rstd = sb("rstd", [P, NB])
        tails = HTx[0:1, 0:2 * TR].rearrange("p (u t) -> p u t", u=2)
        carry = HTx[0:1, 2 * TR:3 * TR + 1]
        cprev = sb("cprev", [P, EB])
        row = HTx[0:1, :]
        bmul = sb("bmul", [3, NB * P])
        degrow = bmul[0:1, :]
        stage = sb("stage", [P, R, CT], i32)
        G = sb("G", [P, R, CT, 2 * F])
        mring = sb("mring", [P, R, CE], bf16)
        ST = sb("ST", [P, 2, CE])
        OSF = sb("OSF", [P, 2, CT, 2 * F])
        OS = OSF[:, :, :, 0:F]
        RB = sb("RB", [P, 2, CE + 1])
        D01 = sb("D01", [P, 2, 2 * CE])
        GZ = VT[:, 0:R * CE].rearrange("p (s k f) -> p s k f", s=R, f=F)
        HM = VT[:, R * CE:(R + 2) * CE].rearrange("p (s e) -> p s e", s=2)
        DN = HT[:, 0:2 * CE].rearrange("p (s e) -> p s e", s=2)
        sring = HT[:, 2 * CE:4 * CE].bitcast(bf16).rearrange("p (s e) -> p s e", s=R)
        M2 = sb("M2", [P, 2, 2, 512])
        Ee, NV = M2[:, 0, :, :], M2[:, 1, :, :]
        big = G[:, :, :, :].rearrange("p a b c -> p (a b c)")
        rgate = D01[:, 0, 0:512]
        omz = D01[:, 0, 512:1024]
        cand = D01[:, 1, 0:512]
        tnh = D01[:, 1, 512:1024]
        WN = big[:, 0:NWB * P].rearrange("p (b c) -> p b c", c=P)
        EV = big[:, 0:2 * 4 * 256].rearrange("p (s k c) -> p s k c", s=2, c=256)
        TF = M2[:, :, :, :].rearrange("p a b c -> p (a b c)")[:, 0:EB * F].rearrange("p (b f) -> p b f", f=F)
        P_t = V[:, 0:EB, :]
        lead = V[:, EB:2 * EB, :]
        fbc = V[:, 2 * EB:3 * EB, :]
        S_t = V[:, 3 * EB:4 * EB, :]
        rows_i = big[:, 0:NB * TILE].rearrange("p (j e) -> p j e", e=TILE).bitcast(i32)
        junk, head_t = (OSF[:, :, :, :].rearrange("p a b c -> p (a b c)")[:, k * TR:(k + 1) * TR].rearrange("p (b e) -> p b e", e=TILE) for k in range(2))
        src_f, first_t = (D01[:, :, :].rearrange("p a b -> p (a b)")[:, k * TR:(k + 1) * TR].rearrange("p (b e) -> p b e", e=TILE) for k in range(2))

        PS = ctx.enter_context(nc.psum_tensor("PS", [P, 8, 512], f32))

        cleared = sem("cleared")
        ld = sem("ld")
        ldw = sem("ldw")
        ldb = sem("ldb")
        pwt = sem("pwt")
        cg = sem("cg")
        dpad = sem("dpad")
        prevld = sem("prevld")
        setup = sem("setup")
        cst2 = sem("cst2")
        cst = sem("cst")
        pst = sem("pst")
        maskst = sem("maskst")
        rowg = sem("rowg")
        wg = sem("wg")
        sq = sem("sq")
        h_ready = sem("h_ready")
        lnv = sem("lnv")
        lns = sem("lns")
        nstep = sem("nstep")
        tr = sem("tr")
        tre = sem("tre")
        v_ready = sem("v_ready")
        a_ready = sem("a_ready")
        agg = [sem(f"agg{g}") for g in range(NG)]
        tabst = sem("tabst")
        attst = [sem(f"attst{q}") for q in range(2)]
        mm = sem("mm")
        mev = sem("mev")
        gr = sem("gr")
        gact = sem("gact")
        gdve = sem("gdve")
        osem = sem("osem")
        zsem = sem("zsem")
        turn = sem("turn")
        staged = sem("staged")
        gath = [sem(f"gath{h}") for h in range(R)]
        scaled = sem("scaled")
        xt = sem("xt")
        scan = sem("scan")
        back = sem("back")
        ev = sem("ev")
        odma = [sem(f"odma{q}") for q in range(2)]
        mld = [sem(f"mld{h}") for h in range(R)]
        ga = sem("ga")
        gv = sem("gv")
        ge = sem("ge")
        gx = sem("gx")
        gfront = sem("gfront")
        gback = sem("gback")
        hm = sem("hm")
        dif = sem("dif")
        dn0 = sem("dn0")
        segm = sem("segm")
        segst = sem("segst")
        tfg = sem("tfg")
        zsc = sem("zsc")
        zt = sem("zt")
        gld = [sem(f"gld{h}") for h in range(R)]
        gstaged = sem("gstaged")
        ggath = [sem(f"ggath{h}") for h in range(R)]
        block = ctx.enter_context(nc.Block())

        SUM = [0, 1, 2, 4]

        BQ, B2 = 0, 384

        def KB(g):
            return min(4, NBR - 4 * g)

        def fori(eng, p, body):
            if p == 0:
                body(0, True)
                with eng.Fori(1, IT) as i:
                    body(i, False)
            else:
                with eng.Fori(0, IT) as i:
                    body(i, False)

        @block.sync
        def _(sp):
            for t in range(2):
                o = t * 13
                sp.dma_start(WN[:, o:o + 4, :], a["L0_gnn_W_msg"][t].rearrange("(q p) (m c) -> p q m c", p=P, c=P)).then_inc(ldw, 16)
                sp.dma_start(WN[:, o + 4:o + 10, :], a["L0_gnn_W_ih"][t].rearrange("(q p) (m c) -> p q m c", p=P, c=P)).then_inc(ldw, 16)
                sp.dma_start(WN[:, o + 10:o + 13, :], a["L0_gnn_W_hh"][t].rearrange("(q p) c -> p q c", p=P)).then_inc(ldw, 16)
                sp.dma_start(bmcol[:, t, :], a["L0_gnn_b_msg"][t].rearrange("(q p) -> p q", p=P), allow_slow_non_contiguous=True).then_inc(ldw, 16)
            for k, s in enumerate(("src", "v", "dst")):
                sp.dma_start(WN[:, 26 + k, :], a[f"L2_gnn_W_{s}"]).then_inc(ldw, 16)
                sp.dma_start(brow[0:1, BQ + k * P:BQ + k * P + P], a[f"L2_gnn_b_{s}"].rearrange("(o f) -> o f", o=1)).then_inc(ldw, 16)
            for k, s in enumerate(("L1_gnn_W", "L3_gnn_W1", "L3_gnn_W_self", "L3_gnn_W_neigh", "L3_gnn_W2")):
                sp.dma_start(WD[:, k, :], a[s]).then_inc(ldw, 16)
            sp.dma_start(brow[0:1, B2:B2 + P], a["L3_gnn_b2"].rearrange("(o f) -> o f", o=1)).then_inc(ldw, 16)
            sp.dma_start(bcol[:, 0:1], a["L3_gnn_b1"].rearrange("(f o) -> f o", o=1)).then_inc(ldw, 16)
            sp.dma_start(bcol[:, 1:2], a["L3_gnn_b_sage"].rearrange("(f o) -> f o", o=1)).then_inc(ldw, 16)
            sp.dma_start(b1bc[:, :], a["L1_gnn_b"].partition_broadcast(P)).then_inc(ldw, 16)
            sp.wait_ge(cleared, 4)
            for t in range(2):
                sp.dma_start(bgate[1:2, t, 0:384], a["L0_gnn_b_ih"][t:t + 1, :]).then_inc(ldb, 16)
                sp.dma_start(bgate[2:3, t, 0:256], a["L0_gnn_b_hh"][t:t + 1, 0:256]).then_inc(ldb, 16)
                sp.dma_start(bgate[2:3, t, 384:512], a["L0_gnn_b_hh"][t:t + 1, 256:384]).then_inc(ldb, 16)
            for tile, name in ((dst_i, "dst"), (src_i, "src"), (w_t, "edge_weight")):
                nfull = FULL // P
                sp.dma_start(tile[:, 0:nfull, :], a[name][0:nfull * P * TILE].rearrange("(b p e) -> p b e", p=P, e=TILE)).then_inc(ld, 16)
                sp.dma_start(tile[0:FULL - nfull * P, nfull, :], a[name][nfull * P * TILE:FULL * TILE].rearrange("(p e) -> p e", e=TILE)).then_inc(ld, 16)
                sp.dma_start(tile[FULL - nfull * P:FULL - nfull * P + 1, nfull, 0:REST], a[name][FULL * TILE:E].rearrange("(o e) -> o e", o=1)).then_inc(ld, 16)
            sp.dma_start(X[:, 0:NBR - 1, :], a["x"][0:(NBR - 1) * P, :].rearrange("(j p) f -> p j f", p=P)).then_inc(ld, 16)
            sp.dma_start(X[0:TAIL, NBR - 1, :], a["x"][(NBR - 1) * P:N, :]).then_inc(ld, 16)
            sp.wait_ge(ld, 16 * 11)
            sp.dma_start(dst_rows[1:TR + 1, :].rearrange("(b p) e -> p b e", p=P), dst_i[:, :, :]).then_inc(dpad, 16)
            sp.dma_start(dst_rows[0:1, :], noprev[:, :]).then_inc(dpad, 16)
            sp.wait_ge(dpad, 32)
            sp.dma_start(prev_i[:, :], dst_rows[0:TR, TILE - 1:TILE].rearrange("(b p) o -> p (b o)", p=P), allow_slow_non_contiguous=True).then_inc(prevld, 16)
            sp.wait_ge(setup, 5)
            sp.dma_start(keep_d.rearrange("(b p e) -> p b e", p=P, e=TILE), keep_t[:, :, :]).then_inc(maskst, 16)
            sp.dma_start(cut_d.rearrange("(b p e) -> p b e", p=P, e=TILE), cut_t[:, :, :]).then_inc(maskst, 16)
            sp.wait_ge(segm, 1)
            sp.dma_start(seg_d.rearrange("(b p e) -> p b e", p=P, e=TILE), seg_t[:, :, :]).then_inc(segst, 16)
            sp.wait_ge(setup, 100)
            sp.dma_start(wsum_d.rearrange("(b p e) o -> p b (e o)", p=P, e=TILE), S_t).then_inc(maskst, 16)

            def prefetch(h, chunk, mask):
                sp.dma_start(mring[:, h, :], mask[bass.ds(chunk * CE, CE)].partition_broadcast(P)).then_inc(mld[h], 16)

            def edge_pass(s, mask, src_ev, src_scan):
                if s == 0:
                    sp.wait_ge(maskst, 48)
                for h in range(R):
                    if s > 0:
                        sp.wait_ge(mld[h], 16 * 50 * s)
                    prefetch(h, h, mask)

                def body(i, first):
                    for h in range(R):
                        c = i * R + h
                        src_ev(c)
                        sp.dma_start(run_d[bass.ds(c * CE, CE), :].rearrange("(k e) f -> e k f", e=TILE),
                                     OS[:, h % 2, :, :]).then_inc(odma[h % 2], 16)
                        src_scan(c)
                        prefetch(h, c + R, mask)
                fori(sp, s, body)

            def att_pass():
                sp.wait_ge(segst, 16)
                for q in range(2):
                    sp.wait_ge(mld[2 * q], 16 * 50 * 3)
                    sp.wait_ge(mld[2 * q + 1], 16 * 50 * 3)

                def load(h, c):
                    at = bass.ds(c * CE, CE)
                    sp.dma_start(GZ[:, h, :, :], run_d[at, :].rearrange("(k e) f -> e k f", e=TILE)).then_inc(gld[h], 16)
                    sp.dma_start(mring[:, h, :], cut_d[at].partition_broadcast(P)).then_inc(gld[h], 16)
                    sp.dma_start(sring[:, h, :], seg_d[at].partition_broadcast(P)).then_inc(gld[h], 16)

                def store(q, c):
                    sp.wait_ge(ev, 3 * NC + c + 1)
                    sp.dma_start(frac_d[bass.ds(c * CE, CE), :].rearrange("(k e) f -> e k f", e=TILE), OSF[:, q, :, :]).then_inc(odma[q], 16)

                for h in range(R):
                    load(h, h)

                def body(i, first, last):
                    for h in range(R):
                        c = i * R + h
                        if not last:
                            sp.wait_ge(dif, c + 1)
                            load(h, c + R)
                        if not (first and h < 2):
                            store(h % 2, c - 2)
                body(0, True, False)
                with sp.Fori(1, IT - 1) as i:
                    body(i, False, False)
                body(IT - 1, False, True)
                for c in (NC - 2, NC - 1):
                    store(c % 2, c)

            for r in range(2):
                sp.wait_ge(h_ready, r + 1)
                sp.dma_start(tabs[r][0:NBR * P, :].rearrange("(j p) f -> p j f", p=P), H[:, 0:NBR, :]).then_inc(tabst, 16)
                edge_pass(r, keep_d, lambda c: sp.wait_ge(ev, r * NC + c + 1), lambda c: sp.wait_ge(scan, r * NC + c + 1))
            sp.wait_ge(mev, MEV_L1)
            sp.dma_start(tabs[2][0:NBR * P, :].rearrange("(j p) f -> p j f", p=P), V[:, 0:NBR, :]).then_inc(tabst, 16)
            edge_pass(2, keep_d, lambda c: sp.wait_ge(ev, 2 * NC + c + 1), lambda c: sp.wait_ge(scan, 2 * NC + c + 1))
            for g in range(NG):
                sp.wait_ge(mev, MEV_L2 + g + 1)
                sp.dma_start(tab_sv[g * 512:g * 512 + KB(g) * P, :].rearrange("(k p) f -> p k f", p=P), EV[:, g % 2, 0:KB(g), :]).then_inc(attst[g % 2], 16)
            sp.dma_start(tab_d[0:NBR * P, :].rearrange("(j p) f -> p j f", p=P), V[:, 0:NBR, :]).then_inc(tabst, 16)
            sp.wait_ge(zsc, 16 * NBR)
            sp.wait_ge(tfg, 16 * EB)
            at_tiles = run_d[0:NC * CE, :].rearrange("(t e) f -> t (e f)", e=TILE)[:, 0:F]
            nf = NC * CT // P
            for b in range(nf):
                sp.dma_start(at_tiles[b * P:(b + 1) * P, :], TF[:, b, :]).then_inc(zt, 16)
            sp.dma_start(at_tiles[nf * P:NC * CT, :], TF[0:NC * CT - nf * P, nf, :]).then_inc(zt, 16)
            sp.wait_ge(zt, 16 * (nf + 1))
            att_pass()
            sp.wait_ge(tre, TRE_H1N)
            sp.dma_start(tabs[3][0:NBR * P, :].rearrange("(j p) f -> p j f", p=P), V[:, 0:NBR, :]).then_inc(tabst, 16)
            edge_pass(3, keep_d, lambda c: sp.wait_ge(ev, 4 * NC + c + 1), lambda c: sp.wait_ge(scan, 3 * NC + c + 1))
            for h in range(R):
                sp.wait_ge(mld[h], 16 * 200)
            sp.wait_ge(osem, 1)
            sp.dma_start(out[0:(NBR - 1) * P, :].rearrange("(j p) f -> p j f", p=P), X[:, 0:NBR - 1, :]).then_inc(zsem, 16)
            sp.dma_start(out[(NBR - 1) * P:N, :], X[0:TAIL, NBR - 1, :]).then_inc(zsem, 16)
            sp.wait_ge(zsem, 32)

        @block.gpsimd
        def _(pool):
            pool.memset(ident[:, :], 0.0).then_inc(cst, 1)
            pool.memset(ones[:, :], 1.0).then_inc(cst, 1)
            pool.memset(nident[:, :], 0.0).then_inc(cst2, 1)
            pool.wait_ge(cst2, 1)
            pool.affine_select(out=nident[:, :], in_=nident[:, :], compare_op=ALU.not_equal, fill=-1.0, base=0,
                               pattern=[[-1, P]], channel_multiplier=1).then_inc(cst2, 1)
            pool.iota(nval_i[:, :], pattern=[[P, NB]], base=0, channel_multiplier=1).then_inc(cst, 1)
            pool.wait_ge(cst, 1)
            pool.affine_select(out=ident[:, :], in_=ident[:, :], compare_op=ALU.not_equal, fill=1.0, base=0,
                               pattern=[[-1, P]], channel_multiplier=1).then_inc(cst, 1)

            def rows_of(dest, table, idx, done):
                pool.indirect_dma_start(dest, None, table, bass.IndirectOffsetOnAxis(ap=idx, axis=0)).then_inc(done, 16)

            pool.wait_ge(dpad, 32)
            pool.wait_ge(cg, 1)
            pool.wait_ge(setup, 7)
            for j in range(NB):
                rows_of(rows_i[:, j, :], dst_rows, trow_i[:, j:j + 1], rowg)
            pool.wait_ge(setup, 102)
            pool.wait_ge(maskst, 48)

            def sum_pass(s, ntab):
                pool.wait_ge(tabst, ntab)

                def body(i, first):
                    for h in range(0, R, 2):
                        pool.wait_ge(staged, s * (NC + R) + i * R + h + 2)
                        pool.sem_inc(turn, 1)
                        for k in range(2 * CT):
                            n = h + k // CT
                            rows_of(G[:, n, k % CT, 0:F], tabs[s], stage[:, n, k % CT:k % CT + 1], gath[n])
                fori(pool, s, body)

            def att_pass():
                pool.wait_ge(mev, MEV_L2 + NG)
                for j in range(NBR):
                    pool.indirect_dma_start(run_d, bass.IndirectOffsetOnAxis(ap=head_i[:, j:j + 1], axis=0), V[:, j, :], None).then_inc(zsc, 16)
                pool.wait_ge(tabst, 64)
                for b in range(EB):
                    rows_of(TF[:, b, :], tab_d, tfirst_i[:, b:b + 1], tfg)
                for q in range(2):
                    pool.wait_ge(attst[q], 16 * ((NG + 1 - q) // 2))

                def body(i, first):
                    for h in range(R):
                        pool.wait_ge(gstaged, i * R + h + 1)
                        pool.sem_inc(turn, 1)
                        for k in range(CT):
                            rows_of(G[:, h, k, :], tab_sv, stage[:, h, k:k + 1], ggath[h])
                fori(pool, 1, body)

            def node_rows(p):
                for q in range(2):
                    pool.wait_ge(odma[q], 16 * (NC // 2) * (p + 1))
                for j in range(NBR):
                    if p == 3:
                        rows_of(AH[:, j, :], frac_d, last_i[:, j:j + 1], agg[j // 4])
                    else:
                        rows_of(A[:, j, :], run_d[0:NC * CE, :], last_i[:, j:j + 1], agg[j // 4])

            sum_pass(0, 16)
            for j in range(NB):
                rows_of(wlast[:, j:j + 1], wsum_d, last_i[:, j:j + 1], wg)
            node_rows(0)
            sum_pass(1, 32)
            node_rows(1)
            sum_pass(2, 48)
            node_rows(2)
            att_pass()
            node_rows(3)
            sum_pass(3, 80)
            node_rows(4)

        @block.tensor
        def _(pe):
            def turn4(bank, blocks):
                for k, b in enumerate(blocks):
                    last = nc.tensor.transpose(PS[:, bank, k * P:(k + 1) * P], b, ident[:, :])
                return last

            state = {"tr": 0}

            def turn_nodes(src):
                for g in range(NG):
                    turn_group(src, g)

            def turn_group(src, g):
                n = state["tr"]
                if n >= 2:
                    pe.wait_ge(tre, n - 1)
                turn4(4 + n % 2, [src(4 * g + k) for k in range(KB(g))]).then_inc(tr, 1)
                state["tr"] += 1

            pe.wait_ge(cst, 4)
            pe.wait_ge(ldw, 16 * 23)
            for g in range(8):
                n = state["tr"]
                if n >= 2:
                    pe.wait_ge(tre, n - 1)
                turn4(4 + n % 2, [WN[:, b, :] for b in range(4 * g, min(4 * g + 4, NWB))]).then_inc(tr, 1)
                state["tr"] += 1
            pe.wait_ge(tre, state["tr"])
            for t in range(2):
                ih = WT[:, t * 13 + 4:t * 13 + 10, :].rearrange("p (q m) c -> p q m c", m=2)
                for half in range(2):
                    for m in range(2):
                        last = nc.tensor.matmul(PS[:, 2 * half + t, 0:384], WN[:, t * 13 + 2 * m + half, :], ih[:, :, m, :], start=m == 0, stop=m == 1)
                for m in range(2):
                    last = nc.tensor.matmul(PS[0:1, 4 + t, 0:384], bmcol[:, t, m:m + 1], ih[:, :, m, :], start=m == 0, stop=m == 1)
            last.then_inc(pwt, 1)
            pe.wait_ge(cg, 1)
            pe.wait_ge(ldb, 96)
            for n, (tab, need) in enumerate(((src_f, 1), (w_t, 1))):
                pe.wait_ge(setup, need)
                pe.wait_ge(ld, 16 * 11)
                b0 = 2 * (n % 2)
                for b in range(EB):
                    last = nc.tensor.transpose(PS[:, b0 + b // 4, (b % 4) * P:(b % 4 + 1) * P], tab[:, b, :], ident[:, :])
                last.then_inc(pst, 1)
            pe.wait_ge(setup, 6)
            for b in range(EB):
                last = nc.tensor.matmul(PS[:, 6 + b // 4, (b % 4) * P:(b % 4 + 1) * P], fbc[:, b, :], ident[:, :], start=True, stop=True)
            last.then_inc(pst, 1)
            pe.wait_ge(setup, 50)
            for u, t in enumerate((P_t, lead)):
                for b in range(EB):
                    last = nc.tensor.matmul(PS[0:1, 6 + b // 4, (b % 4) * P:(b % 4 + 1) * P] if u == 0 else PS[0:1, b // 4, (b % 4) * P:(b % 4 + 1) * P],
                                            t[:, b, P - 1:P], ident[:, :], start=True, stop=True)
            last.then_inc(pst, 1)
            pe.wait_ge(setup, 51)
            for b in range(EB):
                last = nc.tensor.matmul(PS[:, 6, b:b + 1], carry[0:1, b * P:(b + 1) * P], ones[0:1, 0:1], start=True, stop=True)
            last.then_inc(pst, 1)
            pe.wait_ge(setup, 101)
            pe.wait_ge(tre, 8)
            for j in range(NB):
                last = nc.tensor.matmul(PS[0:1, j // 4, (j % 4) * P:(j % 4 + 1) * P], cum[:, j:j + 1], ident[:, :], start=True, stop=True)
            last.then_inc(pst, 1)
            pe.wait_ge(setup, 103)
            for j in range(NB):
                last = nc.tensor.matmul(PS[:, 7, j:j + 1], degrow[0:1, j * P:(j + 1) * P], ones[0:1, 0:1], start=True, stop=True)
            last.then_inc(pst, 1)
            pe.wait_ge(segm, 1)
            for b in range(EB):
                last = nc.tensor.transpose(PS[:, b // 4, (b % 4) * P:(b % 4 + 1) * P], head_t[:, b, :], ident[:, :])
            last.then_inc(pst, 1)
            pe.wait_ge(setup, 104)

            def sum_pass(s, p, weighted):
                C = s * NC
                CA = p * NC

                def body(i, first):
                    for h in range(R):
                        c, q = i * R + h, h % 2
                        if weighted:
                            pe.wait_ge(scaled, c + 1)
                        else:
                            pe.wait_ge(gath[h], 64 * (s * IT + i) + 64)
                        if not (first and h < 2):
                            pe.wait_ge(scan, C + c - 1)
                        turn4(q, [G[:, h, k, 0:F] for k in range(CT)]).then_inc(xt, 1)
                        pe.wait_ge(scan, C + c + 1)
                        if not (first and h < 2):
                            pe.wait_ge(ev, CA + c - 1)
                        turn4(2 + q, [ST[:, q, k * P:(k + 1) * P] for k in range(CT)]).then_inc(back, 1)
                fori(pe, s, body)

            def att_pass():
                pe.wait_ge(cst2, 2)

                def front(i, h, c, young):
                    q = h % 2
                    pe.wait_ge(ggath[h], 64 * i + 64)
                    pe.wait_ge(hm, c + 1)
                    if not young:
                        pe.wait_ge(gfront, GF * (c - 2) + 1)
                    for k in range(CT):
                        o = PS[:, q, k * P:(k + 1) * P]
                        nc.tensor.matmul(o, G[:, h, k, 0:F], ident[:, :], is_transpose=True, start=True, stop=False)
                        last = nc.tensor.matmul(o, GZ[:, h, k, :], HM[:, q, k * P:(k + 1) * P], start=False, stop=True)
                    last.then_inc(ga, 1)

                def values(h, c, young):
                    q = h % 2
                    if not young:
                        pe.wait_ge(gback, GB * (c - 2) + 1)
                    turn4(6 + q, [G[:, h, k, F:2 * F] for k in range(CT)]).then_inc(gv, 1)

                def turn_back(q, c, young):
                    pe.wait_ge(gback, GB * c + GB)
                    pe.wait_ge(ev, 3 * NC + c)
                    turn4(2, [ST[:, q, k * P:(k + 1) * P] for k in range(CT)])
                    turn4(3, [DN[:, q, k * P:(k + 1) * P] for k in range(CT)]).then_inc(back, 1)

                def body(i, first, final):
                    for h in range(R):
                        c, q = i * R + h, h % 2
                        if not (final and h == R - 1):
                            front(i + (h + 1) // R, (h + 1) % R, c + 1, first and h < 1)
                        pe.wait_ge(gfront, GF * c + 3)
                        if not (first and h < 2):
                            pe.wait_ge(gx, c - 1)
                        nc.tensor.matmul(PS[:, 4 + q, :], ident[:, :], RB[:, q, 0:CE], start=True, stop=False)
                        nc.tensor.matmul(PS[:, 4 + q, :], nident[:, :], RB[:, q, 1:CE + 1], start=False, stop=False)
                        nc.tensor.matmul(PS[:, 4 + q, :], identb[:, :], mring[:, h, :], start=False, stop=True).then_inc(dif, 1)
                        if not (final and h == R - 1):
                            values((h + 1) % R, c + 1, first and h < 1)
                        if not (first and h < 2):
                            turn_back(q, c - 2, first)
                front(0, 0, 0, True)
                values(0, 0, True)
                body(0, True, False)
                with pe.Fori(1, IT - 1) as i:
                    body(i, False, False)
                body(IT - 1, False, True)
                for c in (NC - 2, NC - 1):
                    turn_back(c % 2, c, False)

            st = {"mm": 0, "gr": 0}
            for r in range(2):
                o = r * 13
                pe.wait_ge(h_ready, r + 1)
                turn_nodes(lambda b: H[:, b, :])
                pe.wait_ge(v_ready, r + 1)
                turn_nodes(lambda b: V[:, b, :])
                sum_pass(r, r, False)
                hh = WT[:, o + 10:o + 13, :]
                for g in range(NG):
                    pe.wait_ge(agg[g], 16 * KB(g) * (r + 1))
                    turn_group(lambda b: A[:, b, :], g)
                    pe.wait_ge(tre, state["tr"])
                    if st["gr"]:
                        pe.wait_ge(gdve, 2 * st["gr"] - 1)
                    for k in range(KB(g)):
                        n = slice(g * 512 + k * P, g * 512 + (k + 1) * P)
                        nc.tensor.matmul(PS[:, k, :], bmul[:, n], bgate[:, r, :], start=True, stop=False)
                        nc.tensor.matmul(PS[:, k, 0:256], HT[:, n], hh[:, 0:2, :], start=False, stop=False)
                        nc.tensor.matmul(PS[:, k, 384:512], HT[:, n], hh[:, 2, :], start=False, stop=False)
                        nc.tensor.matmul(PS[:, k, 0:384], VT[:, n], US[:, r, 1, :], start=False, stop=False)
                        last = nc.tensor.matmul(PS[:, k, 0:384], AT[:, n], US[:, r, 0, :], start=False, stop=True)
                    last.then_inc(gr, 1)
                    st["gr"] += 1
            pe.wait_ge(h_ready, 3)
            turn_nodes(lambda b: H[:, b, :])
            pe.wait_ge(tre, state["tr"])

            def product(groups, alternate=True):
                for g in range(NG):
                    if g == 0 or not alternate:
                        if st["mm"]:
                            pe.wait_ge(mev, st["mm"])
                    elif g >= 2:
                        pe.wait_ge(mev, st["mm"] - 1)
                    groups(g).then_inc(mm, 1)
                    st["mm"] += 1

            def xw(g):
                for k in range(KB(g)):
                    last = nc.tensor.matmul(PS[:, 6 + g % 2, k * P:(k + 1) * P], HT[:, g * 512 + k * P:g * 512 + (k + 1) * P], WD[:, 0, :], start=True, stop=True)
                return last
            product(xw)
            sum_pass(2, 2, True)
            pe.wait_ge(h_ready, 4)
            turn_nodes(lambda b: H[:, b, :])
            pe.wait_ge(tre, state["tr"])

            def qkv(g):
                for k in range(KB(g)):
                    nc.tensor.matmul(PS[:, k, 0:384], HT[:, g * 512 + k * P:g * 512 + (k + 1) * P], WT[:, 26:29, :], start=True, stop=False)
                    last = nc.tensor.matmul(PS[:, k, 0:384], ones[0:1, :], brow[0:1, BQ:BQ + 384], start=False, stop=True)
                return last
            product(qkv, False)
            pe.wait_ge(mev, st["mm"])
            att_pass()
            pe.wait_ge(h_ready, 5)
            turn_nodes(lambda b: H[:, b, :])
            pe.wait_ge(tre, state["tr"])
            product(lambda g: nc.tensor.matmul(PS[:, 6 + g % 2, 0:KB(g) * P], WD[:, 1, :], HT[:, g * 512:g * 512 + KB(g) * P], start=True, stop=True))
            pe.wait_ge(mev, st["mm"])
            turn_nodes(lambda b: VT[:, b * P:(b + 1) * P])
            assert state["tr"] == TRE_H1N
            sum_pass(3, 4, False)
            pe.wait_ge(a_ready, 1)
            turn_nodes(lambda b: A[:, b, :])
            pe.wait_ge(tre, state["tr"])

            def hidden(g):
                n = slice(g * 512, g * 512 + KB(g) * P)
                nc.tensor.matmul(PS[:, 6 + g % 2, 0:KB(g) * P], WD[:, 2, :], VT[:, n], start=True, stop=False)
                return nc.tensor.matmul(PS[:, 6 + g % 2, 0:KB(g) * P], WD[:, 3, :], AT[:, n], start=False, stop=True)
            product(hidden)
            pe.wait_ge(mev, st["mm"])

            def last_product(g):
                for k in range(KB(g)):
                    nc.tensor.matmul(PS[:, 6 + g % 2, k * P:(k + 1) * P], HT[:, g * 512 + k * P:g * 512 + (k + 1) * P], WD[:, 4, :], start=True, stop=False)
                    last = nc.tensor.matmul(PS[:, 6 + g % 2, k * P:(k + 1) * P], ones[0:1, :], brow[0:1, B2:B2 + P], start=False, stop=True)
                return last
            product(last_product)

        @block.scalar
        def _(act):
            state = {"tr": 0, "mm": 0, "gr": 0}

            def take(dests):
                for d in dests:
                    n = state["tr"]
                    act.wait_ge(tr, n + 1)
                    nc.scalar.activation(d, PS[:, 4 + n % 2, 0:d.free_size()], ACT.Copy).then_inc(tre, 1)
                    state["tr"] += 1

            def groups(t):
                return [t[:, g * 512:g * 512 + KB(g) * P] for g in range(NG)]

            wt = WT[:, :, :].rearrange("p b c -> p (b c)")
            take([wt[:, g * 512:min((g + 1) * 512, NWB * P)] for g in range(8)])
            act.wait_ge(pwt, 1)
            act.wait_ge(cleared, 4)
            for t in range(2):
                for half in range(2):
                    nc.scalar.activation(US[:, t, half, :], PS[:, 2 * half + t, 0:384], ACT.Copy)
                last = nc.scalar.activation(bgate[0:1, t, 0:384], PS[0:1, 4 + t, 0:384], ACT.Copy)
            last.then_inc(cg, 1)

            def ln_sqrt(n):
                act.wait_ge(lnv, n)
                nc.scalar.activation(rstd[:, 0:NBR], tmpn[:, 0:NBR], ACT.Sqrt).then_inc(lns, 1)

            def sum_pass(s, p, weighted):
                CA = p * NC

                def body(i, first):
                    for h in range(R):
                        c, q = i * R + h, h % 2
                        if weighted:
                            act.wait_ge(gath[h], 64 * (s * IT + i) + 64)
                            act.sem_inc(turn, 1)
                            for k in range(CT):
                                last = nc.scalar.activation(G[:, h, k, 0:F], G[:, h, k, 0:F], ACT.Copy, scale=w_e[:, bass.ds(c * CT + k, 1)])
                            last.then_inc(scaled, 1)
                        act.wait_ge(back, CA + c + 1)
                        if not (first and h < 2):
                            act.wait_ge(odma[q], 16 * (p * (NC // 2) + i * 2 + h // 2))
                        nc.scalar.activation(OS[:, q, :, :], PS[:, 2 + q, :].rearrange("p (k f) -> p k f", f=F), ACT.Copy).then_inc(ev, 1)
                fori(act, s, body)

            def att_pass():
                def fifth(q, c, young):
                    act.wait_ge(ga, c + 1)
                    if not young:
                        act.wait_ge(gfront, GF * (c - 2) + GF)
                    nc.scalar.activation(Ee[:, q, :], PS[:, q, :], ACT.Copy, scale=0.2).then_inc(ge, 1)

                def take_out(q, c, k):
                    act.wait_ge(back, 3 * NC + c + 1)
                    act.wait_ge(odma[q], 16 * k)
                    for b, o in ((2, 0), (3, F)):
                        last = nc.scalar.activation(OSF[:, q, :, o:o + F], PS[:, b, :].rearrange("p (k f) -> p k f", f=F), ACT.Copy)
                    last.then_inc(ev, 1)

                def body(i, first, final):
                    for h in range(R):
                        c, q = i * R + h, h % 2
                        if not (final and h == R - 1):
                            fifth(1 - q, c + 1, first and h < 1)
                        act.wait_ge(dif, c + 1)
                        if not (first and h < 2):
                            act.wait_ge(gback, GB * (c - 2) + GB)
                        nc.scalar.activation(D01[:, q, 0:CE], PS[:, 4 + q, :], ACT.Exp)
                        act.wait_ge(gfront, GF * c + GF)
                        nc.scalar.activation(D01[:, q, CE:2 * CE], D01[:, q, CE:2 * CE], ACT.Exp).then_inc(gx, 1)
                        if not (first and h < 2):
                            take_out(q, c - 2, 3 * (NC // 2) + i * 2 + h // 2 - 1)
                fifth(0, 0, True)
                body(0, True, False)
                with act.Fori(1, IT - 1) as i:
                    body(i, False, False)
                body(IT - 1, False, True)
                for c in (NC - 2, NC - 1):
                    take_out(c % 2, c, 4 * (NC // 2) - 1)

            ln_sqrt(1)
            for r in range(2):
                take(groups(HT))
                take(groups(VT))
                sum_pass(r, r, False)
                if r == 0:
                    act.wait_ge(setup, 105)
                    nc.scalar.activation(dis[:, :], tmpn[:, :], ACT.Sqrt).then_inc(sq, 1)
                for g in range(NG):
                    take([groups(AT)[g]])
                    state["gr"] += 1
                    act.wait_ge(gr, state["gr"])
                    if state["gr"] > 1:
                        act.wait_ge(gdve, 2 * (state["gr"] - 1))
                    n = slice(0, KB(g))
                    nc.scalar.activation(rgate.rearrange("p (k c) -> p k c", c=P)[:, n, :], PS[:, n, 0:128], ACT.Sigmoid)
                    nc.scalar.activation(omz.rearrange("p (k c) -> p k c", c=P)[:, n, :], PS[:, n, 128:256], ACT.Sigmoid, scale=-1.0).then_inc(gact, 1)
                    act.wait_ge(gdve, 2 * state["gr"] - 1)
                    nc.scalar.activation(tnh[:, 0:KB(g) * P], cand[:, 0:KB(g) * P], ACT.Tanh).then_inc(gact, 1)
            ln_sqrt(2)
            take(groups(HT))
            for g in range(NG):
                act.wait_ge(mm, state["mm"] + 1)
                for k in range(KB(g)):
                    last = nc.scalar.activation(V[:, 4 * g + k, :], PS[:, 6 + g % 2, k * P:(k + 1) * P], ACT.Copy, scale=dis[:, 4 * g + k:4 * g + k + 1])
                last.then_inc(mev, 1)
                state["mm"] += 1
            assert state["mm"] == MEV_L1
            sum_pass(2, 2, True)
            ln_sqrt(3)
            take(groups(HT))
            for g in range(NG):
                act.wait_ge(mm, state["mm"] + 1)
                if g >= 2:
                    act.wait_ge(attst[g % 2], 16 * (g // 2))
                n = KB(g)
                nc.scalar.activation(EV[:, g % 2, 0:n, :], PS[:, 0:n, 0:256], ACT.Copy)
                nc.scalar.activation(V[:, 4 * g:4 * g + n, :], PS[:, 0:n, 256:384], ACT.Copy).then_inc(mev, 1)
                state["mm"] += 1
            att_pass()
            ln_sqrt(4)
            take(groups(HT))
            for g in range(NG):
                act.wait_ge(mm, state["mm"] + 1)
                nc.scalar.activation(groups(VT)[g], PS[:, 6 + g % 2, 0:KB(g) * P], ACT.Relu, bias=bcol[:, 0:1]).then_inc(mev, 1)
                state["mm"] += 1
            take([V[:, 4 * g:4 * g + KB(g), :] for g in range(NG)])
            sum_pass(3, 4, False)
            take(groups(AT))
            for g in range(NG):
                act.wait_ge(mm, state["mm"] + 1)
                nc.scalar.activation(groups(HT)[g], PS[:, 6 + g % 2, 0:KB(g) * P], ACT.Relu, bias=bcol[:, 1:2]).then_inc(mev, 1)
                state["mm"] += 1
            for g in range(NG):
                act.wait_ge(mm, state["mm"] + 1)
                nc.scalar.activation(H[:, 4 * g:4 * g + KB(g), :], PS[:, 6 + g % 2, 0:KB(g) * P].rearrange("p (k c) -> p k c", c=P), ACT.Relu).then_inc(mev, 1)
                state["mm"] += 1

        @block.vector
        def _(dve):
            chain = {"n": 0}

            def step(ins):
                chain["n"] += 1
                ins.then_inc(nstep, 1)
                dve.wait_ge(nstep, chain["n"])

            v = nc.vector
            v.memset(dst_i[:, :, :], NONE)
            v.memset(src_i[:, :, :], 0)
            v.memset(noprev[:, :], -1)
            v.memset(w_t[:, :, :], 0.0).then_inc(cleared, 2)
            step(v.memset(onesb[:, :], 1.0))
            step(v.memset(bmul[:, :], 1.0))
            step(v.memset(bgate[:, :, :], 0.0))
            v.memset(X[:, NBR - 1:NB, :], 0.0).then_inc(cleared, 2)
            step(v.memset(carry[:, 0:1], 0.0))
            step(v.memset(zero[:, :], 0.0))
            step(v.memset(ST[:, :, :], 0.0))
            step(v.memset(RB[:, :, :], 0.0))
            dve.wait_ge(cleared, 4)
            dve.wait_ge(ld, 16 * 11)
            v.tensor_copy(src_f, src_i[:, :, :]).then_inc(setup, 1)
            step(v.tensor_copy(dst_f[:, :, :], dst_i[:, :, :]))
            step(v.tensor_scalar(prev_f[:, :], dst_f[:, :, 0], float(NBR * P - 1), None, ALU.min))
            step(v.tensor_copy(tfirst_i[:, :], prev_f[:, :]))
            dve.wait_ge(cst, 4)
            dve.wait_ge(pst, 1)
            pv = PS[:, :, :].rearrange("p b c -> p (b c)")
            v.tensor_copy(src_e[:, :], pv[:, 0:TR]).then_inc(setup, 3)
            step(v.tensor_copy(identb[:, :], ident[:, :]))
            dve.wait_ge(prevld, 16)
            step(v.tensor_copy(prev_f[:, :], prev_i[:, :]))
            v.tensor_tensor(keep_t[:, :, 1:TILE], dst_f[:, :, 1:TILE], dst_f[:, :, 0:TILE - 1], ALU.is_equal)
            step(v.tensor_tensor(keep_t[:, :, 0], dst_f[:, :, 0], prev_f[:, :], ALU.is_equal))
            v.tensor_scalar(cut_t[:, :, :], keep_t[:, :, :], BIG, -BIG, ALU.mult, ALU.add).then_inc(setup, 1)
            v.tensor_copy(fbc, dst_f[:, :, 0:1].to_broadcast([P, EB, P])).then_inc(setup, 1)
            def bc(t):
                return t[:, 0:NBR].unsqueeze(2).to_broadcast([P, NBR, F])

            def layernorm(n):
                x, c, h = X[:, 0:NBR, :], A[:, 0:NBR, :], H[:, 0:NBR, :]
                step(v.tensor_reduce(mean[:, 0:NBR], x, AX.X, ALU.add))
                step(v.tensor_scalar(mean[:, 0:NBR], mean[:, 0:NBR], 1.0 / F, None, ALU.mult))
                step(v.tensor_tensor(c, x, bc(mean), ALU.subtract))
                step(v.tensor_tensor(h, c, c, ALU.mult))
                step(v.tensor_reduce(tmpn[:, 0:NBR], h, AX.X, ALU.add))
                v.tensor_scalar(tmpn[:, 0:NBR], tmpn[:, 0:NBR], 1.0 / F, EPS, ALU.mult, ALU.add).then_inc(lnv, 1)
                dve.wait_ge(lns, n)
                step(v.reciprocal(rstd[:, 0:NBR], rstd[:, 0:NBR]))
                v.scalar_tensor_tensor(h, c, 0.0, bc(rstd), ALU.max, ALU.mult).then_inc(h_ready, 1)

            step(v.tensor_copy(nval[:, :], nval_i[:, :]))
            step(v.tensor_scalar(src_f, keep_t[:, :, :], -1.0, 1.0, ALU.mult, ALU.add))
            step(v.memset(src_f[:, :, 0], 0.0))
            for b in range(EB):
                step(v.tensor_tensor_scan(first_t[:, b, :], onesb[:, :], src_f[:, b, :], 0.0, ALU.mult, ALU.add))
            step(v.tensor_copy(seg_t[:, :, :], first_t))
            step(v.memset(src_f[:, :, 0], 1.0))
            step(v.scalar_tensor_tensor(head_t, first_t, 1.0, src_f, ALU.add, ALU.mult))
            v.tensor_scalar(head_t, head_t, -1.0, None, ALU.add).then_inc(segm, 1)
            dve.wait_ge(pst, 2)
            step(v.tensor_copy(w_e[:, :], pv[:, 1024:1024 + TR]))
            dve.wait_ge(pst, 3)
            for j in range(NB):
                step(v.tensor_scalar(junk, pv[:, 3072:3072 + TR].rearrange("p (b e) -> p b e", e=TILE), nval[:, j:j + 1], 0.0, ALU.is_le, ALU.add, accum_out=cnt[:, j:j + 1]))
            step(v.tensor_scalar(trow[:, :], cnt[:, :], 1.0, 1.0, ALU.max, ALU.mult))
            v.tensor_copy(trow_i[:, :], trow[:, :]).then_inc(setup, 1)
            for b in range(EB):
                v.tensor_tensor_scan(P_t[:, b, :], keep_t[:, b, :], w_t[:, b, :], 0.0, ALU.mult, ALU.add)
                last = v.tensor_tensor_scan(lead[:, b, :], keep_t[:, b, :], zero[:, :], 1.0, ALU.mult, ALU.add)
            last.then_inc(setup, 43)
            layernorm(1)
            dve.wait_ge(pst, 4)
            v.tensor_copy(tails[:, 0, :], pv[0:1, 3072:3072 + TR])
            step(v.tensor_copy(tails[:, 1, :], pv[0:1, 0:TR]))
            v.tensor_tensor_scan(carry[:, 1:TR + 1], tails[:, 1, :], tails[:, 0, :], 0.0, ALU.mult, ALU.add).then_inc(setup, 1)
            dve.wait_ge(pst, 5)
            step(v.tensor_copy(cprev[:, :], PS[:, 6, 0:EB]))
            for b in range(EB):
                last = v.scalar_tensor_tensor(S_t[:, b, :], lead[:, b, :], cprev[:, b:b + 1], P_t[:, b, :], ALU.mult, ALU.add)
            last.then_inc(setup, 49)
            dve.wait_ge(rowg, 16 * NB)
            for j in range(NB):
                step(v.tensor_scalar(junk[:, 0, :], rows_i[:, j, :], nval[:, j:j + 1], 0.0, ALU.is_le, ALU.add, accum_out=cnt2[:, j:j + 1]))
            step(v.tensor_scalar(trow[:, :], trow[:, :], -1.0, float(TILE), ALU.add, ALU.mult))
            v.tensor_tensor(cum[:, :], trow[:, :], cnt2[:, :], ALU.add).then_inc(setup, 1)
            dve.wait_ge(setup, 101)
            step(v.tensor_scalar(trow[:, :], cum[:, :], -1.0, 0.0, ALU.add, ALU.max))
            v.tensor_copy(last_i[:, :], trow[:, :]).then_inc(setup, 1)
            dve.wait_ge(pst, 6)
            step(v.memset(row[:, 0:1], 0.0))
            step(v.tensor_copy(row[:, 1:NB * P + 1], pv[0:1, 0:NB * P]))
            v.tensor_tensor(degrow[:, :], row[:, 1:NB * P + 1], row[:, 0:NB * P], ALU.subtract).then_inc(setup, 1)
            dve.wait_ge(pst, 7)
            v.tensor_copy(deg[:, :], PS[:, 7, 0:NB]).then_inc(setup, 1)
            dve.wait_ge(setup, 104)
            step(v.tensor_scalar(has[:, :], deg[:, :], 1.0, None, ALU.min))
            step(v.tensor_tensor(cum[:, :], cum[:, :], deg[:, :], ALU.subtract))
            step(v.tensor_scalar(trow[:, :], nval[:, :], float(NC * CE), None, ALU.add))
            step(v.tensor_tensor(cum[:, :], cum[:, :], trow[:, :], ALU.subtract))
            step(v.tensor_tensor(cum[:, :], cum[:, :], has[:, :], ALU.mult))
            step(v.tensor_tensor(cum[:, :], cum[:, :], trow[:, :], ALU.add))
            step(v.tensor_copy(head_i[:, :], cum[:, :]))
            dve.wait_ge(pst, 8)
            step(v.tensor_copy(head_e[:, :], pv[:, 0:TR]))
            step(v.tensor_scalar(invdeg[:, :], deg[:, :], 1.0, None, ALU.max))
            step(v.reciprocal(invdeg[:, :], invdeg[:, :]))
            step(v.tensor_tensor(invdeg[:, :], invdeg[:, :], has[:, :], ALU.mult))
            def gathered(p):
                for g in range(NG):
                    dve.wait_ge(agg[g], 16 * KB(g) * p)

            def stage_ahead(h, tile, done):
                v.tensor_scalar(stage[:, h, :], src_e[:, bass.ds(tile, CT)], 0.0, None, ALU.add).then_inc(done, 1)

            def sum_pass(s, p):
                C = s * NC
                if s:
                    dve.wait_ge(staged, s * (NC + R))
                for h in range(R):
                    stage_ahead(h, h * CT, staged)

                def body(i, first):
                    for h in range(R):
                        c, q = i * R + h, h % 2
                        dve.wait_ge(mld[h], 16 * (50 * s + i) + 16)
                        dve.wait_ge(xt, C + c + 1)
                        if not (first and h < 2):
                            dve.wait_ge(back, p * NC + c - 1)
                        if not (first and h < 1):
                            dve.wait_ge(scan, C + c)
                        v.tensor_tensor_scan(ST[:, q, :], mring[:, h, :], PS[:, q, :], ST[:, 1 - q, CE - 1:CE], ALU.mult, ALU.add).then_inc(scan, 1)
                        stage_ahead(h, (c + R) * CT, staged)
                fori(dve, s, body)

            def att_pass():
                dve.wait_ge(staged, 3 * (NC + R))
                dve.wait_ge(tre, TRE_L2)
                dve.wait_ge(mm, MEV_L2 + NG)
                for h in range(R):
                    stage_ahead(h, h * CT, gstaged)
                v.memset(DN, 0.0).then_inc(dn0, 1)
                dve.wait_ge(dn0, 1)

                def heads(i, h, c):
                    dve.wait_ge(gld[h], 48 * i + 48)
                    v.tensor_tensor(HM[:, h % 2, :].rearrange("p (k e) -> p k e", e=TILE),
                                    sring[:, h, :].rearrange("p (k e) -> p k e", e=TILE),
                                    head_e[:, bass.ds(c * CT, CT)].unsqueeze(2).to_broadcast([P, CT, TILE]),
                                    ALU.is_equal).then_inc(hm, 1)

                def weighted(h, c):
                    q = h % 2
                    dve.wait_ge(gx, c + 1)
                    dve.wait_ge(gv, c + 1)
                    v.tensor_tensor(NV[:, q, :], D01[:, q, CE:2 * CE], PS[:, 6 + q, :], ALU.mult).then_inc(gback, 1)

                def denominator(h, c, young, chunk0, final):
                    q = h % 2
                    if not young:
                        dve.wait_ge(back, 3 * NC + c - 1)
                    if not chunk0:
                        dve.wait_ge(gback, GB * c)
                    v.tensor_tensor_scan(DN[:, q, :], D01[:, q, 0:CE], D01[:, q, CE:2 * CE], DN[:, 1 - q, CE - 1:CE], ALU.mult, ALU.add).then_inc(gback, 1)
                    if not final:
                        stage_ahead(h, (c + R) * CT, gstaged)

                def numerator(h, c):
                    q = h % 2
                    dve.wait_ge(gback, GB * c + 1)
                    v.tensor_tensor_scan(ST[:, q, :], D01[:, q, 0:CE], NV[:, q, :], ST[:, 1 - q, CE - 1:CE], ALU.mult, ALU.add).then_inc(gback, 1)

                def body(i, first, final):
                    for h in range(R):
                        c, q, hb = i * R + h, h % 2, (h - 1) % R
                        has_back = not (first and h < 1)
                        dve.wait_ge(ge, c + 1)
                        v.tensor_tensor(Ee[:, q, :], PS[:, q, :], Ee[:, q, :], ALU.max).then_inc(gfront, 1)
                        v.tensor_copy(RB[:, q, 0:1], RB[:, 1 - q, CE:CE + 1]).then_inc(gfront, 1)
                        dve.wait_ge(gfront, GF * c + 2)
                        v.tensor_tensor_scan(RB[:, q, 1:CE + 1], mring[:, h, :], Ee[:, q, :], RB[:, q, 0:1], ALU.add, ALU.max).then_inc(gfront, 1)
                        if has_back:
                            weighted(hb, c - 1)
                        dve.wait_ge(gfront, GF * c + 3)
                        v.tensor_tensor(D01[:, q, CE:2 * CE], Ee[:, q, :], RB[:, q, 1:CE + 1], ALU.subtract).then_inc(gfront, 1)
                        if has_back:
                            denominator(hb, c - 1, first and h < 3, first and h < 2, final and h > 0)
                        if not (final and h >= 2):
                            heads(i + (h + 2) // R, (h + 2) % R, c + 2)
                        if has_back:
                            numerator(hb, c - 1)
                heads(0, 0, 0)
                heads(0, 1, 1)
                body(0, True, False)
                with dve.Fori(1, IT - 1) as i:
                    body(i, False, False)
                body(IT - 1, False, True)
                weighted((NC - 1) % R, NC - 1)
                denominator((NC - 1) % R, NC - 1, False, False, True)
                numerator((NC - 1) % R, NC - 1)

            st = {"gr": 0}
            for r in range(2):
                dve.wait_ge(h_ready, r + 1)
                if r == 0:
                    dve.wait_ge(maskst, 48)
                else:
                    dve.wait_ge(tre, 8 + 3 * NG)
                v.tensor_tensor(V[:, 0:NBR, :], H[:, 0:NBR, :], bc(deg), ALU.mult).then_inc(v_ready, 1)
                sum_pass(r, r)
                if r == 0:
                    dve.wait_ge(wg, 16 * NB)
                    step(v.tensor_tensor(wlast[:, :], wlast[:, :], has[:, :], ALU.mult))
                    step(v.tensor_scalar(wlast[:, :], wlast[:, :], 1.0, None, ALU.add))
                    step(v.tensor_scalar(tmpn[:, :], wlast[:, :], 1e-30, None, ALU.max))
                    v.reciprocal(tmpn[:, :], tmpn[:, :]).then_inc(setup, 1)
                    step(v.tensor_scalar(wlast[:, :], wlast[:, :], 0.0, None, ALU.is_gt))
                    dve.wait_ge(sq, 1)
                    step(v.tensor_tensor(dis[:, :], dis[:, :], wlast[:, :], ALU.mult))
                dve.wait_ge(tabst, 16 * (r + 1))
                for g in range(NG):
                    n = st["gr"]
                    kk = slice(4 * g, 4 * g + KB(g))
                    dve.wait_ge(gact, 2 * n + 1)
                    cd = cand.rearrange("p (k c) -> p k c", c=P)[:, 0:KB(g), :]
                    tn = tnh.rearrange("p (k c) -> p k c", c=P)[:, 0:KB(g), :]
                    oz = omz.rearrange("p (k c) -> p k c", c=P)[:, 0:KB(g), :]
                    step(v.tensor_tensor(cd, rgate.rearrange("p (k c) -> p k c", c=P)[:, 0:KB(g), :], PS[:, 0:KB(g), 384:512], ALU.mult))
                    v.tensor_tensor(cd, cd, PS[:, 0:KB(g), 256:384], ALU.add).then_inc(gdve, 1)
                    dve.wait_ge(gact, 2 * n + 2)
                    step(v.tensor_tensor(tn, tn, H[:, kk, :], ALU.subtract))
                    step(v.tensor_tensor(tn, tn, oz, ALU.mult))
                    step(v.tensor_tensor(tn, tn, has[:, kk].unsqueeze(2).to_broadcast([P, KB(g), F]), ALU.mult))
                    v.tensor_tensor(H[:, kk, :], H[:, kk, :], tn, ALU.add).then_inc(gdve, 1)
                    st["gr"] += 1
                dve.wait_ge(gdve, 2 * st["gr"])
                if r == 0:
                    dve.sem_inc(h_ready, 1)
            step(v.tensor_tensor(X[:, 0:NBR, :], X[:, 0:NBR, :], H[:, 0:NBR, :], ALU.add))
            layernorm(2)
            dve.wait_ge(h_ready, 3)

            sum_pass(2, 2)
            gathered(3)
            dve.wait_ge(tabst, 48)
            r_ = slice(0, NBR)
            step(v.tensor_tensor(A[:, r_, :], A[:, r_, :], bc(has), ALU.mult))
            step(v.tensor_tensor(A[:, r_, :], A[:, r_, :], V[:, r_, :], ALU.add))
            step(v.tensor_tensor(A[:, r_, :], A[:, r_, :], bc(dis), ALU.mult))
            step(v.tensor_tensor(A[:, r_, :], A[:, r_, :], b1bc[:, :].unsqueeze(1).to_broadcast([P, NBR, F]), ALU.add))
            step(v.tensor_tensor(X[:, r_, :], X[:, r_, :], A[:, r_, :], ALU.add))
            layernorm(3)
            dve.wait_ge(h_ready, 4)

            att_pass()
            gathered(4)
            step(v.reciprocal(H[:, r_, :], H[:, r_, :]))
            step(v.tensor_tensor(A[:, r_, :], A[:, r_, :], H[:, r_, :], ALU.mult))
            step(v.tensor_tensor(A[:, r_, :], A[:, r_, :], bc(has), ALU.mult))
            step(v.tensor_tensor(X[:, r_, :], X[:, r_, :], A[:, r_, :], ALU.add))
            layernorm(4)
            dve.wait_ge(h_ready, 5)

            sum_pass(3, 4)
            gathered(5)
            v.tensor_tensor(A[:, r_, :], A[:, r_, :], bc(invdeg), ALU.mult).then_inc(a_ready, 1)
            dve.wait_ge(mev, MEV_L1 + 4 * NG)
            v.tensor_tensor(X[:, r_, :], X[:, r_, :], H[:, r_, :], ALU.add).then_inc(osem, 1)


MEV_L1 = NG
MEV_L2 = NG
TRE_H1N = 8 + 10 * NG
TRE_L2 = 8 + 8 * NG
GF, GB = 4, 3


_INS = ["x", "src", "dst", "edge_weight", "L0_gnn_W_msg", "L0_gnn_b_msg", "L0_gnn_W_ih", "L0_gnn_W_hh",
        "L0_gnn_b_ih", "L0_gnn_b_hh", "L1_gnn_W", "L1_gnn_b", "L2_gnn_W_src", "L2_gnn_b_src", "L2_gnn_W_dst",
        "L2_gnn_b_dst", "L2_gnn_W_v", "L2_gnn_b_v", "L3_gnn_W1", "L3_gnn_b1", "L3_gnn_W_self",
        "L3_gnn_W_neigh", "L3_gnn_b_sage", "L3_gnn_W2", "L3_gnn_b2"]


def kernel(**inputs):
    import numpy as np
    import concourse.bacc as bacc
    from concourse.bass_utils import run_bass_kernel_spmd

    nc = bacc.Bacc("TRN2", target_bir_lowering=False, num_devices=1)
    arrays, aps = {}, {}
    for name in _INS:
        arrays["in_" + name] = np.ascontiguousarray(inputs[name])
        aps[name] = nc.dram_tensor("in_" + name, arrays["in_" + name].shape,
                                   mybir.dt.from_np(arrays["in_" + name].dtype), kind="ExternalInput").ap()
    out = nc.dram_tensor("out", (N, F), mybir.dt.float32, kind="ExternalOutput").ap()
    build(nc, aps, out)
    r = run_bass_kernel_spmd(nc, [arrays], core_ids=[0])
    return r.results[0]["out"]
```
